# Optimizing a Trainium2 kernel written in Bass

```python
import numpy as np
import jax
import jax.numpy as jnp

def _softmax(x, axis=-1):
    return jax.nn.softmax(x, axis=axis)

def _gelu(x):
    return jax.nn.gelu(x, approximate=True)

def _silu(x):
    return jax.nn.silu(x)

def _sigmoid(x):
    return jax.nn.sigmoid(x)

def _layernorm(x, axis=-1, eps=1e-05):
    m = jnp.mean(x, axis=axis, keepdims=True)
    v = jnp.var(x, axis=axis, keepdims=True)
    return (x - m) / jnp.sqrt(v + eps)

def _scatter_add(tgt, idx, src, axis=0):
    return tgt.at[idx].add(src)

def _segment_sum(src, seg, n):
    return jax.ops.segment_sum(src, seg, n)
kernel_name = 'mk_xattn_ffn_d1_seqx_r4_db7af0'

def setup_inputs(seed: int=0):
    np.random.seed(seed)
    _w = jnp.asarray

    def _rec_inputs():
        import jax
        import jax.numpy as jnp
        _rk = jax.random.key(seed)
        x = -0.0005207 + 1.001 * jax.random.normal(jax.random.fold_in(_rk, 1), (8, 256, 256), jnp.float32)
        _lenS = 256 - jax.random.randint(jax.random.fold_in(_rk, 7), (8,), 0, max(1, 256 // 4) + 1, jnp.int32)
        _lenS2 = 77 - jax.random.randint(jax.random.fold_in(_rk, 8), (8,), 0, max(1, 77 // 4) + 1, jnp.int32)
        _ctx_1024P = jax.random.normal(jax.random.fold_in(_rk, 11), (8, 16, 256), jnp.float32)
        _ctx_1024c = jax.random.dirichlet(jax.random.fold_in(_rk, 511), 0.3 * jnp.ones((16,), jnp.float32), (8, 77))
        _ctx_1024t = jnp.einsum('bsk,bkd->bsd', _ctx_1024c, _ctx_1024P)
        _ctx_1024t = _ctx_1024t * jax.lax.rsqrt(jnp.mean(jnp.square(_ctx_1024t)) + 1e-12) * 0.953939
        ctx_1024 = -1.39393e-06 + 0.999914 * (_ctx_1024t + 0.3 * jax.random.normal(jax.random.fold_in(_rk, 611), (8, 77, 256), jnp.float32))
        itok_BxS_0_1023 = jax.random.randint(jax.random.fold_in(_rk, 12), (8, 256), 0, 256, jnp.int32)
        itok_BxS2_0_2047 = jax.random.randint(jax.random.fold_in(_rk, 13), (8, 77), 0, 512, jnp.int32)
        return (x, ctx_1024, itok_BxS_0_1023, itok_BxS2_0_2047)
    x, ctx_1024, itok_BxS_0_1023, itok_BxS2_0_2047 = _rec_inputs()

    def _L0_xattn_setup():
        import jax, jax.numpy as jnp
        import numpy as np
        DIM = 256
        H = 16
        HD = DIM // H
        SCALE = HD ** (-0.5)
        LAMBDA_INIT = 0.1
        EPS = 1e-06

        def _split_heads(x, B, N):
            return x.reshape(B, N, H, HD).transpose(0, 2, 1, 3)
        key0 = jax.random.key(seed)
        ks = jax.random.split(key0, 12)
        B, Nq, Nk = (2, 256, 512)
        w = 0.02
        inp = {'query': jax.random.normal(ks[0], (B, Nq, DIM), jnp.float32), 'key': jax.random.normal(ks[1], (B, Nk, DIM), jnp.float32), 'value': jax.random.normal(ks[2], (B, Nk, DIM), jnp.float32), 'qpos': jax.random.randint(ks[3], (B, Nq), 0, Nq, jnp.int32), 'kpos': jax.random.randint(ks[4], (B, Nk), 0, Nk, jnp.int32), 'q1_w': jax.random.normal(ks[5], (DIM, DIM), jnp.float32) * w, 'q2_w': jax.random.normal(ks[6], (DIM, DIM), jnp.float32) * w, 'kv1_w': jax.random.normal(ks[7], (2 * DIM, DIM), jnp.float32) * w, 'kv2_w': jax.random.normal(ks[8], (2 * DIM, DIM), jnp.float32) * w, 'proj_w': jax.random.normal(ks[9], (DIM, DIM), jnp.float32) * w, 'proj_b': jnp.zeros((DIM,), jnp.float32), 'norm_w': jnp.ones((DIM,), jnp.float32), 'lambda_1': jnp.ones((1, H, 1, 1), jnp.float32), 'lambda_2': jnp.full((1, H, 1, 1), 1.0 - LAMBDA_INIT * (1.0 / 12.0), jnp.float32)}
        return inp
    _L0_xattn_all = _L0_xattn_setup()
    _L0_xattn_in = {k: v for k, v in _L0_xattn_all.items() if k in ('q1_w', 'q2_w', 'kv1_w', 'kv2_w', 'proj_w', 'proj_b', 'norm_w', 'lambda_1', 'lambda_2')}
    del _L0_xattn_all

    def _L0_ffn_setup():
        import jax, jax.numpy as jnp
        import numpy as np
        TOP_K = 2
        key = jax.random.key(seed)
        k1, k2, k3, k4 = jax.random.split(key, 4)
        B, S, H, I, E = (2, 512, 256, 1024, 8)
        return {'hidden_states': jax.random.normal(k1, (B, S, H), jnp.float32), 'gate_w': jax.random.normal(k2, (E, H), jnp.float32) * 0.02, 'gate_up_proj': jax.random.normal(k3, (E, 2 * I, H), jnp.float32) * 0.02, 'down_proj': jax.random.normal(k4, (E, H, I), jnp.float32) * 0.02}
    _L0_ffn_all = _L0_ffn_setup()
    _L0_ffn_in = {k: v for k, v in _L0_ffn_all.items() if k in ('gate_w', 'gate_up_proj', 'down_proj')}
    del _L0_ffn_all
    return {'x': x, 'ctx_1024': ctx_1024, 'itok_BxS_0_1023': itok_BxS_0_1023, 'itok_BxS2_0_2047': itok_BxS2_0_2047, 'L0_xattn_q1_w': _L0_xattn_in['q1_w'], 'L0_xattn_q2_w': _L0_xattn_in['q2_w'], 'L0_xattn_kv1_w': _L0_xattn_in['kv1_w'], 'L0_xattn_kv2_w': _L0_xattn_in['kv2_w'], 'L0_xattn_proj_w': _L0_xattn_in['proj_w'], 'L0_xattn_proj_b': _L0_xattn_in['proj_b'], 'L0_xattn_norm_w': _L0_xattn_in['norm_w'], 'L0_xattn_lambda_1': _L0_xattn_in['lambda_1'], 'L0_xattn_lambda_2': _L0_xattn_in['lambda_2'], 'L0_ffn_gate_w': _L0_ffn_in['gate_w'], 'L0_ffn_gate_up_proj': _L0_ffn_in['gate_up_proj'], 'L0_ffn_down_proj': _L0_ffn_in['down_proj']}

def reference(x, ctx_1024, itok_BxS_0_1023, itok_BxS2_0_2047, L0_xattn_q1_w, L0_xattn_q2_w, L0_xattn_kv1_w, L0_xattn_kv2_w, L0_xattn_proj_w, L0_xattn_proj_b, L0_xattn_norm_w, L0_xattn_lambda_1, L0_xattn_lambda_2, L0_ffn_gate_w, L0_ffn_gate_up_proj, L0_ffn_down_proj):
    import jax
    import jax.numpy as jnp

    def _L0_xattn_ref(query, key, value, qpos, kpos, q1_w, q2_w, kv1_w, kv2_w, proj_w, proj_b, norm_w, lambda_1, lambda_2):
        import jax, jax.numpy as jnp
        import numpy as np
        DIM = 256
        H = 16
        HD = DIM // H
        SCALE = HD ** (-0.5)
        LAMBDA_INIT = 0.1
        EPS = 1e-06

        def _split_heads(x, B, N):
            return x.reshape(B, N, H, HD).transpose(0, 2, 1, 3)
        B, Nq, C = query.shape
        Nk = key.shape[1]
        q1 = _split_heads(query @ q1_w.T, B, Nq)
        q2 = _split_heads(query @ q2_w.T, B, Nq)
        kv1 = (key @ kv1_w.T).reshape(B, Nk, 2, H, HD).transpose(2, 0, 3, 1, 4)
        k1, v1 = (kv1[0], kv1[1])
        kv2 = (key @ kv2_w.T).reshape(B, Nk, 2, H, HD).transpose(2, 0, 3, 1, 4)
        k2 = kv2[0]
        attn1 = jax.nn.softmax(jnp.einsum('bhqd,bhkd->bhqk', q1, k1) * SCALE, axis=-1)
        attn2 = jax.nn.softmax(jnp.einsum('bhqd,bhkd->bhqk', q2, k2) * SCALE, axis=-1)
        lambda_full = lambda_1 - lambda_2 + LAMBDA_INIT
        diff_attn = attn1 - lambda_full * attn2
        x = jnp.einsum('bhqk,bhkd->bhqd', diff_attn, v1)
        x = x.transpose(0, 2, 1, 3).reshape(B, Nq, C)
        xf = x.astype(jnp.float32)
        xf = xf * jax.lax.rsqrt(jnp.mean(xf * xf, axis=-1, keepdims=True) + EPS) * norm_w
        x = xf.astype(x.dtype)
        return x @ proj_w.T + proj_b

    def _L0_ffn_ref(hidden_states, gate_w, gate_up_proj, down_proj):
        import jax, jax.numpy as jnp
        import numpy as np
        TOP_K = 2
        B, S, H = hidden_states.shape
        E = gate_w.shape[0]
        x = hidden_states.reshape(-1, H)
        T = x.shape[0]
        probs = jax.nn.softmax(x @ gate_w.T, axis=-1)
        w, idx = jax.lax.top_k(probs, TOP_K)
        w = w / jnp.sum(w, axis=-1, keepdims=True)
        combine = jnp.zeros((T, E), x.dtype).at[jnp.arange(T)[:, None], idx].add(w)

        def step(acc, inputs):
            gup, dn, ce = inputs
            g, u = jnp.split(x @ gup.T, 2, axis=-1)
            acc = acc + ce[:, None] * (jax.nn.silu(g) * u @ dn.T)
            return (acc, None)
        out, _ = jax.lax.scan(step, jnp.zeros_like(x), (gate_up_proj, down_proj, combine.T))
        return out.reshape(B, S, H)
    x = x + _L0_xattn_ref(_layernorm(x, axis=-1), ctx_1024, ctx_1024, itok_BxS_0_1023, itok_BxS2_0_2047, L0_xattn_q1_w, L0_xattn_q2_w, L0_xattn_kv1_w, L0_xattn_kv2_w, L0_xattn_proj_w, L0_xattn_proj_b, L0_xattn_norm_w, L0_xattn_lambda_1, L0_xattn_lambda_2)
    x = x + _L0_ffn_ref(_layernorm(x, axis=-1), L0_ffn_gate_w, L0_ffn_gate_up_proj, L0_ffn_down_proj)
    return x

_drawn_inputs = setup_inputs


def setup_inputs(seed=0):
    import zlib

    import numpy as np

    out = dict(_drawn_inputs(seed))
    spreads = {'L0_xattn_proj_b': (0.0, 0.1),
     'L0_xattn_norm_w': (1.0, 0.2),
     'L0_xattn_lambda_1': (1.0, 0.2),
     'L0_xattn_lambda_2': (0.9916666746139526, 0.2)}
    factors = {'L0_xattn_q1_w': 3.952,
     'L0_xattn_q2_w': 8.0,
     'L0_xattn_kv2_w': 8.0,
     'L0_ffn_gate_w': 7.746}
    for name, (base, spread) in spreads.items():
        noise = np.random.default_rng([zlib.crc32(name.encode()), seed]).standard_normal(out[name].shape)
        drawn = base * np.exp(spread * noise) if base else spread * noise
        out[name] = jnp.asarray(drawn.astype(out[name].dtype))
    for name, factor in factors.items():
        out[name] = (out[name] * factor).astype(out[name].dtype)
    return out
```

```python
from contextlib import ExitStack

import numpy as np

import concourse.bass as bass
from concourse import mybir

F32 = mybir.dt.float32
BF16 = mybir.dt.bfloat16
F16 = mybir.dt.float16
I32 = mybir.dt.int32
U32 = mybir.dt.uint32
ALU = mybir.AluOpType
ACT = mybir.ActivationFunctionType
AX = mybir.AxisListType

P = 128
B, S, D = 8, 256, 256
SK = 77
H, HD = 16, 16
E, FF = 8, 1024
T = B * S
TT = T // P
TPB = S // P
KC = D // P
FC = FF // P
NT = (2 * T + E * (P - 1)) // P
NTP = NT
SCALE = HD ** -0.5
VW = HD + 1
W1N, W2N = KC * 2 * FF, FC * D
EW = 2 * (W1N + W2N)
CH = 1024
NCH = (W1N + W2N) // CH
EARLY = 4
STG = 2
CPB = EARLY * NCH // B


def at_start(n):
    return isinstance(n, int) and n <= 0


def moe_attention_kernel(nc, x, ctxT, wqT, wkT, wvT, projT, proj_b, norm_w, lam1, lam2, gateT, w1, w2, out):
    ctx = ExitStack()
    with ctx:
        def sb(name, shape, dt):
            return ctx.enter_context(nc.sbuf_tensor(name, shape, dt))

        def sem(name):
            return ctx.enter_context(nc.semaphore(name))

        WE = sb("WE", [P, E, EW], BF16)
        FB = sb("FB", [P, 15360 // 2], BF16)
        ident = sb("ident", [P, P], BF16)
        slot_tok = sb("slot_tok", [P, NTP], I32)
        slot_w = sb("slot_w", [P, NTP], F32)
        idx_now = sb("idx_now", [P, 3], I32)
        idx_g, idx_s = [idx_now[:, 0:1], idx_now[:, 1:2]], idx_now[:, 2:3]
        pause = sb("pause", [P, 2], BF16)
        tile_exp = sb("tile_exp", [1, NTP], I32)

        def carver(flat, limit):
            at = [0]

            def take(n, dt=F32, parts=P):
                size = n * (2 if dt in (BF16, F16) else 4) // 2
                size += size % 2
                v = flat[0:parts, at[0]:at[0] + size]
                at[0] += size
                assert at[0] <= limit, (at[0], limit)
                return v if dt == BF16 else v.bitcast(dt)
            return take

        late = WE[:, EARLY:E, :].rearrange("p e n -> p (e n)")
        tail = late[:, 3 * EW:4 * EW]
        big = carver(late, 3 * EW)
        att = carver(FB[:, :], 3072)
        setup = carver(tail, EW)

        qst = [big(H * S, BF16).rearrange("p (h q) -> p h q", h=H) for _ in range(2)]
        kst = [big(H * 2 * SK, BF16).rearrange("p (h n) -> p h n", h=H) for _ in range(2)]
        VWP = H * VW + 16
        vp = big(B * VWP).rearrange("p (b n) -> p b n", b=B)
        wq_sb = big(KC * 2 * D).rearrange("p (k n) -> p k n", k=KC)
        pj_sb = big(KC * D).rearrange("p (k n) -> p k n", k=KC)
        ots = big(4 * 512).rearrange("p (g n) -> p g n", g=4)
        pr = [big(512) for _ in range(2)]
        xn = att(TPB * D).rearrange("p (t n) -> p t n", t=TPB)
        xnT = att(KC * S).rearrange("p (k n) -> p k n", k=KC)
        qh = att(4 * S, BF16).rearrange("p (m n) -> p m n", m=4)
        ql = big(4 * S, BF16).rearrange("p (m n) -> p m n", m=4)
        xa = big(TPB * D).rearrange("p (t n) -> p t n", t=TPB)
        xd = big(TPB * D).rearrange("p (t n) -> p t n", t=TPB)
        bias_bc = big(D)
        mT = big(S, BF16)
        o_sb = big(TPB * D).rearrange("p (t n) -> p t n", t=TPB)
        xmid = big(TPB * D).rearrange("p (t n) -> p t n", t=TPB)
        x2 = big(TPB * D).rearrange("p (t n) -> p t n", t=TPB)
        x2s = big(TPB * 2 * D, BF16).rearrange("p (t s n) -> p t s n", t=TPB, s=2)
        identf = big(P)
        gate_sb = big(KC * E).rearrange("p (k n) -> p k n", k=KC)
        mx = big(TPB * 2 * H).rearrange("p (t h a) -> p t h a", t=TPB, a=2)
        mneg = big(TPB * 2 * 2 * H, BF16).rearrange("p (t s a h) -> p t s a h", t=TPB, s=2, a=2)
        bn = big(TPB * 2 * 6).rearrange("p (w t n) -> p w t n", w=2, t=TPB)
        mv = big(TPB * 2 * 2).rearrange("p (w t n) -> p w t n", w=2, t=TPB)
        veps = big(TPB * 3).rearrange("p (w t) -> p w t", w=3)
        rstd = big(TPB * 3).rearrange("p (w t) -> p w t", w=3)
        sumsq = big(TPB)
        rc = big(2 * H).rearrange("p (a h) -> p a h", a=2)
        lams = big(3 * H).rearrange("p (a h) -> p a h", a=3)
        normw = big(KC)
        negh = big(2)
        logits = setup(TT * E).rearrange("p (t e) -> p t e", t=TT)
        wk_sb = setup(KC * 2 * D).rearrange("p (k n) -> p k n", k=KC)
        wv_sb = setup(KC * D).rearrange("p (k n) -> p k n", k=KC)
        ctx_sb = setup(KC * B * SK).rearrange("p (k n) -> p k n", k=KC)
        kh = setup(4 * B * SK, BF16).rearrange("p (m n) -> p m n", m=4)
        kl = setup(4 * B * SK, BF16).rearrange("p (m n) -> p m n", m=4)
        after = carver(tail, 2 * TT * E + 2 * KC * 3 * D)
        after(TT * E)
        o_b = after(TPB * D).rearrange("p (t n) -> p t n", t=TPB)
        oT, x2T, sq_junk = after(KC * P), after(KC * P), after(D)

        rt = carver(tail, EW)
        rt(TT * E)
        oneh = rt(2 * TT * P, F16).rearrange("p (j n) -> p j n", j=2 * TT)
        rtab = rt(2 * TT * 4 * NTP, F16).rearrange("p (j k n) -> p j k n", j=2 * TT, k=4)
        te = lambda v: v.rearrange("p (t e) -> p t e", t=TT)
        et = lambda v: v.rearrange("p (e t) -> p e t", e=E)
        r_eq, r_key, r_two = te(rt(TT * E)), te(rt(TT * E)), te(rt(TT * E))
        r_oh = [te(rt(TT * E)) for _ in range(2)]
        r_tot, r_inc, r_slot, r_reset = (et(rt(TT * E)) for _ in range(4))
        sm = carver(FB[:, :], 3072)
        r_rank = te(sm(TT * E))
        r_iota = sm(P)
        r_tok = sm(TT)
        r_pad = sm(1)
        r_mask = et(sm(TT * E, BF16))
        r_before, r_ones = sm(P, BF16), sm(P, BF16)
        r_m1, r_m2, r_top, r_diff, r_exp = (sm(TT) for _ in range(5))
        r_w = sm(2 * TT)
        r_wh, r_wl = sm(2 * TT, F16), sm(2 * TT, F16)
        r_sl, r_tile, r_pos = sm(2 * TT), sm(2 * TT), sm(2 * TT)
        r_sli, r_tilei, r_posi = sm(2 * TT, I32), sm(2 * TT, I32), sm(2 * TT, I32)
        r_cnt, r_cnti, r_cntj, r_nt, r_end, r_base, r_one8 = sm(E), sm(E, I32), sm(E, I32), sm(E), sm(E), sm(E), sm(E)
        r_tab = sm(4 * NTP).rearrange("p (k n) -> p k n", k=4)
        r_free = sm(NTP)
        r_exf = sm(NTP)
        rcmp = sm(NTP * E)

        ffb = carver(FB[:, :], 7680)
        xg = [ffb(2 * D, BF16) for _ in range(2)]
        xgT = [ffb(2 * D, BF16).rearrange("p (c n) -> p c n", c=4) for _ in range(2)]
        sil = ffb(512)
        hs = [ffb(1024, BF16).rearrange("p (s n) -> p s n", s=2) for _ in range(2)]
        hT = [ffb(1024, BF16).rearrange("p (c n) -> p c n", c=8) for _ in range(2)]
        y_sb = ffb(D)
        stage = [FB[:, 3072 + 2 * CH * n:3072 + 2 * CH * (n + 1)].bitcast(F32) for n in range(STG)]

        bank = [ctx.enter_context(nc.psum_tensor(f"bank{i}", [P, 512], F32)) for i in range(8)]
        sc_bank, st_bank, ot_bank = bank[0:2], bank[2:4], bank[4:6]
        A6, A7 = bank[6], bank[7]

        QROWS = 2 * HD + 2
        qd = [nc.dram_tensor(f"q_parts{p}", [2, QROWS, H, S], BF16, kind="Internal").ap() for p in range(2)]
        kd = nc.dram_tensor("k_parts", [2, 2 * HD, H, B * SK], BF16, kind="Internal").ap()
        xs = nc.dram_tensor("x_parts", [T + P, 2 * D], BF16, kind="Internal").ap()

        const_ready = sem("const_ready")
        ctx_in = sem("ctx_in")
        kvw_in = sem("kvw_in")
        wq_in = sem("wq_in")
        smalls_in = sem("smalls_in")
        zq_out = sem("zq_out")
        pads_out = sem("pads_out")
        kv_mm = sem("kv_mm")
        kh_ready = sem("kh_ready")
        kl_ready = sem("kl_ready")
        kd_out = sem("kd_out")
        kst_in = sem("kst_in")
        v_mm = sem("v_mm")
        v_ready = sem("v_ready")
        setup_dve = sem("setup_dve")
        xa_in = sem("xa_in")
        ln1_stats = sem("ln1_stats")
        ln1_var = sem("ln1_var")
        ln1_rstd = sem("ln1_rstd")
        xn_ready = sem("xn_ready")
        xt_mm = sem("xt_mm")
        xnT_ready = sem("xnT_ready")
        q_mm = sem("q_mm")
        qh_ready = sem("qh_ready")
        ql_ready = sem("ql_ready")
        qd_out = sem("qd_out")
        qst_in = sem("qst_in")
        sc_mm = sem("sc_mm")
        mx_ready = sem("mx_ready")
        mneg_ready = sem("mneg_ready")
        mt_mm = sem("mt_mm")
        mT_ready = sem("mT_ready")
        m_in = sem("m_in")
        st_mm = sem("st_mm")
        p_ready = sem("p_ready")
        pv_mm = sem("pv_mm")
        ots_ready = sem("ots_ready")
        dt_mm = sem("dt_mm")
        o_ready = sem("o_ready")
        ss_ready = sem("ss_ready")
        rms_var = sem("rms_var")
        rms_ready = sem("rms_ready")
        otr_mm = sem("otr_mm")
        oT_ready = sem("oT_ready")
        pj_mm = sem("pj_mm")
        xd_in = sem("xd_in")
        xm1_ready = sem("xm1_ready")
        xm_ready = sem("xm_ready")
        ln2_stats = sem("ln2_stats")
        ln2_var = sem("ln2_var")
        ln2_rstd = sem("ln2_rstd")
        x2_ready = sem("x2_ready")
        x2h_ready = sem("x2h_ready")
        x2l_ready = sem("x2l_ready")
        x2t_mm = sem("x2t_mm")
        x2T_ready = sem("x2T_ready")
        lg_mm = sem("lg_mm")
        lg_ready = sem("lg_ready")
        w_hi = sem("w_hi")
        w_lo = sem("w_lo")
        route_d = sem("route_d")
        route_a = sem("route_a")
        route_m = sem("route_m")
        route_t = sem("route_t")
        route_mm = sem("route_mm")
        idx_ready = sem("idx_ready")
        idxg_ready = sem("idxg_ready")
        idxs_ready = sem("idxs_ready")
        rconst_ready = sem("rconst_ready")
        xgt_mm = sem("xgt_mm")
        xgT_ready = sem("xgT_ready")
        g_mm = sem("g_mm")
        sil_ready = sem("sil_ready")
        h_ready = sem("h_ready")
        hi_ready = sem("hi_ready")
        lo_ready = sem("lo_ready")
        ht_mm = sem("ht_mm")
        hT_ready = sem("hT_ready")
        y_mm = sem("y_mm")
        y_ready = sem("y_ready")
        y_out = sem("y_out")
        dve_step = sem("dve_step")
        pool_step = sem("pool_step")
        xm_out = [sem(f"xm_out{p}") for p in range(2)]
        x2_out = [sem(f"x2_out{p}") for p in range(2)]
        stage_in = [sem(f"stage_in{p}") for p in range(2)]
        xg_in = [sem(f"xg_in{p}") for p in range(2)]

        block = ctx.enter_context(nc.Block())

        STEPS = {0: [("XT", 0), ("DT", 0)], 1: [("Q", 0)], 2: [("OT", 0)], 3: [("DT", 1)], 4: [("PJ", 0)],
                 5: [("OT", 1)], 6: [("SC", 0), ("SC", 1)], 7: [("SC", 2), ("PJ", 1)], 8: [("SC", 3), ("X2", 0), ("SC", 4)],
                 9: [("SC", 5), ("SC", 6)], 10: [("X2", 1), ("SC", 7)], 11: [("LG", 0), ("SC", 8)],
                 12: [("SC", 9), ("SC", 10)], 13: [("LG", 1), ("SC", 11)], 14: [("MT", 0)], 15: []}
        WSTEP = {2: 0, 7: 1, 12: 2}
        NEXT = ("XT", "Q", "SC", "MT")

        def steps(b, h):
            for kind, i in STEPS[h]:
                bb = b + 1 if kind in NEXT else b - 1
                if 0 <= bb < B:
                    yield kind, i, bb

        def score_group(g):
            t, u = g // 6, g % 6
            return t, range(3 * u, min(3 * u + 3, H))

        def piece(n):
            e, c = n // NCH, n % NCH
            if c < W1N // CH:
                return w1[e, :, c * CH:(c + 1) * CH], WE[:, e, c * CH:(c + 1) * CH], WE[:, e, W1N + c * CH:W1N + (c + 1) * CH]
            c -= W1N // CH
            o = 2 * W1N + c * CH
            return w2[e, :, c * CH:(c + 1) * CH], WE[:, e, o:o + CH], WE[:, e, o + W2N:o + W2N + CH]

        @block.sync
        def _(sp):
            for k in range(KC):
                sp.dma_start(wk_sb[:, k, :], wkT[k * P:(k + 1) * P, :]).then_inc(kvw_in, 16)
                sp.dma_start(ctx_sb[:, k, :], ctxT[k * P:(k + 1) * P, :]).then_inc(ctx_in, 16)
                sp.dma_start(wv_sb[:, k, :], wvT[k * P:(k + 1) * P, :]).then_inc(kvw_in, 16)
            for k in range(KC):
                sp.dma_start(wq_sb[:, k, :], wqT[k * P:(k + 1) * P, :]).then_inc(wq_in, 16)
                sp.dma_start(pj_sb[:, k, :], projT[k * P:(k + 1) * P, :]).then_inc(smalls_in, 16)
                sp.dma_start(gate_sb[:, k, :], gateT[k * P:(k + 1) * P, :]).then_inc(smalls_in, 16)
                sp.dma_start(normw[:, k:k + 1], norm_w[k * P:(k + 1) * P, :]).then_inc(smalls_in, 16)
            sp.dma_start(bias_bc, proj_b.partition_broadcast(P)).then_inc(smalls_in, 16)
            sp.dma_start(lams[:, 0, :], lam1.partition_broadcast(P)).then_inc(smalls_in, 16)
            sp.dma_start(lams[:, 1, :], lam2.partition_broadcast(P)).then_inc(smalls_in, 16)

            def load_x(b):
                if 2 * b > 0:
                    sp.wait_ge(xn_ready, 2 * b)
                sp.dma_start(xa, x[b * S:(b + 1) * S, :].rearrange("(t p) n -> p t n", p=P)).then_inc(xa_in, 16)

            def load_piece(n):
                if n >= STG:
                    sp.wait_ge(w_lo, n - STG + 1)
                sp.dma_start(stage[n % STG], piece(n)[0]).then_inc(stage_in[n % STG], 16)

            load_x(0)
            for n in range(STG):
                load_piece(n)
            sp.wait_ge(const_ready, 6)
            zrow = kst[0].rearrange("p h n -> p (h n)")
            sp.dma_start(xs[T:T + P, :], zrow[:, 0:2 * D]).then_inc(pads_out, 16)
            sp.dma_start(out[T:T + P, :], zrow[:, 0:2 * D].bitcast(F32)).then_inc(pads_out, 16)
            for p in range(2):
                for a in range(2):
                    sp.dma_start(qd[p][a, 2 * HD:QROWS, :, :].rearrange("r h q -> r (h q)"),
                                 qst[0][0:2].rearrange("p h q -> p (h q)")).then_inc(zq_out, 16)
            sp.wait_ge(kl_ready, 4)
            for a in range(2):
                for part, t_ in ((0, kh), (1, kl)):
                    for half in range(2):
                        dst = kd[a, part * HD:(part + 1) * HD, half * 8:(half + 1) * 8, :].rearrange("d j n -> j d n")
                        sp.dma_start(dst, t_[:, 2 * a + half, :]).then_inc(kd_out, 16)

            def load_k(b):
                sp.wait_ge(kd_out, 16 * 8)
                sp.wait_ge(setup_dve, 4)
                if b >= 2:
                    sp.wait_ge(st_mm, H * (b - 1))
                for a in range(2):
                    for r, part in ((0, 0), (1, 1), (2, 0)):
                        p0 = 64 * a + HD * r
                        sp.dma_start(kst[b % 2][p0:p0 + HD, :, a * SK:(a + 1) * SK],
                                     kd[a, part * HD:(part + 1) * HD, :, b * SK:(b + 1) * SK]).then_inc(kst_in, 16)

            def queries(b):
                sp.wait_ge(ql_ready, 2 * b + 2)
                if b >= 2:
                    sp.wait_ge(qst_in, 96 * (b - 1))
                for a in range(2):
                    for part, t_ in ((0, qh), (1, ql)):
                        for half in range(2):
                            dst = qd[b % 2][a, part * HD:(part + 1) * HD, half * 8:(half + 1) * 8, :].rearrange("d j n -> j d n")
                            sp.dma_start(dst, t_[:, 2 * a + half, :]).then_inc(qd_out, 16)
                load_k(b)
                sp.wait_ge(qd_out, 128 * (b + 1))
                sp.wait_ge(zq_out, 64)
                for a in range(2):
                    for r, r0, n in ((0, 0, HD), (1, 0, HD), (2, HD, HD + 2)):
                        p0 = 64 * a + HD * r
                        sp.dma_start(qst[b % 2][p0:p0 + n, :, :], qd[b % 2][a, r0:r0 + n, :, :]).then_inc(qst_in, 16)

            def shifts(b):
                sp.wait_ge(mT_ready, b + 1)
                for a in range(2):
                    for part in range(2):
                        p0 = part * 32 + a * H
                        sp.dma_start(qst[b % 2][64 * a + 48 + part:64 * a + 49 + part, :, :], mT[p0:p0 + H, :]).then_inc(m_in, 16)

            queries(0)
            load_x(1)
            shifts(0)
            for b in range(B + 1):
                for h in range(H):
                    if b < B and h in WSTEP:
                        n = CPB * b + WSTEP[h] + STG
                        if n < E * NCH:
                            load_piece(n)
                    for kind, i, bb in steps(b, h):
                        if kind == "Q":
                            queries(bb)
                            if bb + 1 < B:
                                load_x(bb + 1)
                        if kind == "MT":
                            shifts(bb)
                        if kind == "DT" and i == 0:
                            if bb >= 1:
                                if 2 * bb > 0:
                                    sp.wait_ge(xm1_ready, 2 * bb)
                            sp.dma_start(xd, x[bb * S:(bb + 1) * S, :].rearrange("(t p) n -> p t n", p=P)).then_inc(xd_in, 16)
                        if kind == "X2":
                            r = bb * S + i * P
                            sp.wait_ge(xm_ready, 2 * bb + i + 1)
                            sp.dma_start(out[r:r + P, :], xmid[:, i, :]).then_inc(xm_out[i], 16)
                        if kind == "LG":
                            r = bb * S + i * P
                            sp.wait_ge(x2l_ready, 2 * bb + i + 1)
                            sp.dma_start(xs[r:r + P, :], x2s[:, i].rearrange("p s n -> p (s n)")).then_inc(x2_out[i], 16)
            sp.wait_ge(lg_ready, TT)
            for i in range(TPB):
                sp.wait_ge(xm_out[i], 16 * B)
                sp.wait_ge(x2_out[i], 16 * B)
            for n in range(EARLY * NCH + STG, E * NCH):
                load_piece(n)

        @block.gpsimd
        def _(pool):
            pool_count = [0]

            def step(ins, n=pool_count):
                ins.then_inc(pool_step, 1)
                n[0] += 1
                pool.wait_ge(pool_step, n[0])

            step(nc.gpsimd.memset(identf, 0.0))
            step(nc.gpsimd.affine_select(out=identf, in_=identf, compare_op=ALU.not_equal, fill=1.0, base=0,
                                         pattern=[[-1, P]], channel_multiplier=1))
            nc.gpsimd.tensor_copy(ident[:, :], identf).then_inc(const_ready, 1)
            nc.gpsimd.memset(negh, -0.5).then_inc(const_ready, 1)

            def lo_part(n):
                _, hi, lo = piece(n)
                pool.wait_ge(w_hi, n + 1)
                nc.gpsimd.tensor_tensor(lo, stage[n % STG], hi, ALU.subtract).then_inc(w_lo, 1)

            def power(w, t0, n, src, src_sem, count, mul, var_sem, done):
                pool.wait_ge(src_sem, count)
                eps = 1e-6 if w == 2 else 1e-5
                nc.gpsimd.tensor_scalar(veps[:, w, t0:t0 + n], src, mul, eps, ALU.mult, ALU.add).then_inc(var_sem, 1)
                return eps

            step(nc.gpsimd.memset(pause[:, :], 0.0))

            def rsqrt(w, t, src, src_sem, var_sem, done, k):
                power(w, t, 1, src, src_sem, k + 1, 1.0 / D if w == 2 else 1.0, var_sem, done)
                pool.wait_ge(var_sem, k + 1)
                nc.gpsimd.tensor_tensor(rstd[:, w, t:t + 1], veps[:, w, t:t + 1], negh[:, 0:1], ALU.pow).then_inc(done, 1)

            def ln1(b):
                for t in range(TPB):
                    rsqrt(0, t, mv[:, 0, t, 1:2], ln1_stats, ln1_var, ln1_rstd, TPB * b + t)

            ln1(0)
            for b in range(B + 1):
                for h in range(H):
                    for kind, i, bb in steps(b, h):
                        if kind == "XT":
                            ln1(bb)
                        if kind == "OT":
                            rsqrt(2, i, sumsq[:, i:i + 1], ss_ready, rms_var, rms_ready, TPB * bb + i)
                        if kind == "PJ":
                            rsqrt(1, i, mv[:, 1, i, 1:2], ln2_stats, ln2_var, ln2_rstd, TPB * bb + i)
                    if b < B and h in WSTEP:
                        lo_part(CPB * b + WSTEP[h])
            pool.wait_ge(lg_ready, TT)
            nc.gpsimd.iota(r_rank, [[0, TT], [-1, E]], base=E, channel_multiplier=0, allow_small_or_imprecise_dtypes=True).then_inc(rconst_ready, 1)
            nc.gpsimd.iota(r_iota, [[1, P]], base=0, channel_multiplier=0, allow_small_or_imprecise_dtypes=True).then_inc(rconst_ready, 1)
            nc.gpsimd.iota(r_tok, [[P, TT]], base=0, channel_multiplier=1, allow_small_or_imprecise_dtypes=True).then_inc(rconst_ready, 1)
            nc.gpsimd.iota(r_pad, [[0, 1]], base=T, channel_multiplier=1, allow_small_or_imprecise_dtypes=True).then_inc(rconst_ready, 1)
            step(nc.gpsimd.memset(r_ones, 1.0), pool_count)
            nc.gpsimd.affine_select(out=r_before, in_=r_ones, compare_op=ALU.is_gt, fill=0.0, base=0,
                                    pattern=[[1, P]], channel_multiplier=-1).then_inc(rconst_ready, 1)
            for n in range(EARLY * NCH, E * NCH):
                lo_part(n)

            pool.wait_ge(idx_ready, 1)

            def gather(i, p):
                if not isinstance(i, int) or i >= 2:
                    if not at_start(i - 1):
                        pool.wait_ge(xgt_mm, i - 1)
                nc.gpsimd.tensor_copy(idx_g[p][:, :], slot_tok[:, bass.ds(i, 1)]).then_inc(idxg_ready, 1)
                pool.wait_ge(idxg_ready, i + 1)
                nc.gpsimd.tensor_tensor(pause[:, 0:1], pause[:, 1:2], pause[:, 1:2], ALU.add)
                pool.indirect_dma_start(out=xg[p], out_offset=None, in_=xs,
                                        in_offset=bass.IndirectOffsetOnAxis(ap=idx_g[p][:, 0:1].bitcast(U32), axis=0),
                                        ).then_inc(xg_in[p], 16)

            def scatter(i, p):
                pool.wait_ge(y_ready, i + 1)
                if not at_start(16 * i):
                    pool.wait_ge(y_out, 16 * i)
                nc.gpsimd.tensor_copy(idx_s[:, :], slot_tok[:, bass.ds(i, 1)]).then_inc(idxs_ready, 1)
                pool.wait_ge(idxs_ready, i + 1)
                nc.gpsimd.tensor_tensor(pause[:, 0:1], pause[:, 1:2], pause[:, 1:2], ALU.add)
                pool.indirect_dma_start(out=out, out_offset=bass.IndirectOffsetOnAxis(ap=idx_s[:, 0:1].bitcast(U32), axis=0),
                                        in_=y_sb, in_offset=None, compute_op=ALU.add).then_inc(y_out, 16)

            def turn(i, p, more=True):
                if more:
                    gather(i + 2, p)
                scatter(i, p)

            gather(0, 0)
            gather(1, 1)
            turn(0, 0)
            turn(1, 1)
            turn(2, 0)
            with pool.Fori(1, (NT - 3) // 2) as j:
                turn(2 * j + 1, 1)
                turn(2 * j + 2, 0)
            turn(NT - 2, 1, False)
            turn(NT - 1, 0, False)
            pool.wait_ge(y_out, 16 * NT)

        @block.scalar
        def _(act):
            for m in range(4):
                act.wait_ge(kv_mm, m + 1)
                for n in range(2):
                    w = B * SK // 2
                    nc.scalar.activation(kh[:, m, n * w:(n + 1) * w], bank[2 * (m % 2) + n][:, 0:w], ACT.Copy, scale=SCALE).then_inc(kh_ready, 1)

            def hi_part(n):
                act.wait_ge(stage_in[n % STG], 16 * (n // STG + 1))
                nc.scalar.activation(piece(n)[1], stage[n % STG], ACT.Copy).then_inc(w_hi, 1)

            def xnT_copy(b):
                act.wait_ge(xt_mm, b + 1)
                if 2 * b > 0:
                    act.wait_ge(q_mm, 2 * b)
                nc.scalar.activation(xnT.rearrange("p k n -> p (k n)"), A6[:, :], ACT.Copy).then_inc(xnT_ready, 1)

            def q_hi(b):
                for a, A in ((0, A6), (1, A7)):
                    act.wait_ge(q_mm, 2 * b + a + 1)
                    if 128 * b > 0:
                        act.wait_ge(qd_out, 128 * b)
                    nc.scalar.activation(qh[:, 2 * a:2 * a + 2, :].rearrange("p m n -> p (m n)"), A[:, :], ACT.Copy).then_inc(qh_ready, 1)

            def mt_copy(b):
                act.wait_ge(mt_mm, b + 1)
                if 64 * b > 0:
                    act.wait_ge(m_in, 64 * b)
                nc.scalar.activation(mT[0:64, :], A6[0:64, 0:S // 2].bitcast(BF16), ACT.Copy).then_inc(mT_ready, 1)

            def exp(b, h):
                n = b * H + h
                act.wait_ge(st_mm, n + 1)
                if n - 1 > 0:
                    act.wait_ge(pv_mm, n - 1)
                nc.scalar.activation(pr[h % 2][0:SK, :], st_bank[h % 2][0:SK, :], ACT.Exp).then_inc(p_ready, 1)

            xnT_copy(0)
            q_hi(0)
            mt_copy(0)
            exp(0, 0)
            for b in range(B + 1):
                for h in range(H):
                    if b < B and (b, h) != (B - 1, H - 1):
                        exp(b + (h + 1) // H, (h + 1) % H)
                    for kind, i, bb in steps(b, h):
                        n = TPB * bb + i
                        if kind == "XT":
                            xnT_copy(bb)
                        if kind == "Q":
                            q_hi(bb)
                        if kind == "MT":
                            mt_copy(bb)
                        if kind == "OT":
                            act.wait_ge(o_ready, n + 1)
                            nc.scalar.activation(sq_junk, o_sb[:, i, :], ACT.Square, accum_out=sumsq[:, i:i + 1]).then_inc(ss_ready, 1)
                            act.wait_ge(otr_mm, n + 1)
                            if n > 0:
                                act.wait_ge(pj_mm, n)
                            nc.scalar.activation(oT, A6[:, 0:KC * P], ACT.Copy).then_inc(oT_ready, 1)
                        if kind == "X2":
                            act.wait_ge(x2_ready, n + 1)
                            if 16 * bb > 0:
                                act.wait_ge(x2_out[i], 16 * bb)
                            nc.scalar.activation(x2s[:, i, 0, :], x2[:, i, :], ACT.Copy).then_inc(x2h_ready, 1)
                            act.wait_ge(x2t_mm, n + 1)
                            if n > 0:
                                act.wait_ge(lg_mm, n)
                            nc.scalar.activation(x2T, A6[:, 0:KC * P], ACT.Copy).then_inc(x2T_ready, 1)
                    if b < B and h in WSTEP:
                        hi_part(CPB * b + WSTEP[h])
            act.wait_ge(route_d, 1)
            nc.scalar.activation(r_exp, r_diff, ACT.Exp).then_inc(route_a, 1)
            for n in range(EARLY * NCH, E * NCH):
                if n == (E - 1) * NCH:
                    act.wait_ge(idx_ready, 1)
                hi_part(n)

            def xgT_copy(i, p):
                act.wait_ge(xgt_mm, i + 1)
                nc.scalar.activation(xgT[p].rearrange("p c n -> p (c n)"), A6[:, 0:256].bitcast(BF16), ACT.Copy).then_inc(xgT_ready, 1)

            def hT_copy(k, n):
                act.wait_ge(ht_mm, k + 1)
                nc.scalar.activation(hT[n].rearrange("p c n -> p (c n)"), bank[4 + n][:, :].bitcast(BF16), ACT.Copy).then_inc(hT_ready, 1)

            def gate(k, n):
                act.wait_ge(g_mm, k + 1)
                if not at_start(k):
                    act.wait_ge(lo_ready, k)
                nc.scalar.activation(sil, bank[2 * n][:, :], ACT.Silu).then_inc(sil_ready, 1)
                act.wait_ge(h_ready, k + 1)
                if not at_start(k - 1):
                    act.wait_ge(ht_mm, k - 1)
                nc.scalar.activation(hs[n][:, 0, :], sil, ACT.Copy).then_inc(hi_ready, 1)

            def turn(i, p, first=False, last=False):
                gate(2 * i, 0)
                if not first:
                    hT_copy(2 * i - 1, 1)
                gate(2 * i + 1, 1)
                hT_copy(2 * i, 0)
                if not last:
                    xgT_copy(i + 1, 1 - p)

            act.wait_ge(w_lo, E * NCH)
            xgT_copy(0, 0)
            turn(0, 0, first=True)
            turn(1, 1)
            turn(2, 0)
            with act.Fori(1, (NT - 3) // 2) as j:
                turn(2 * j + 1, 1)
                turn(2 * j + 2, 0)
            turn(NT - 2, 1)
            turn(NT - 1, 0, last=True)
            hT_copy(2 * NT - 1, 1)

        @block.vector
        def _(dve):
            count = [0]

            def step(ins):
                count[0] += 1
                ins.then_inc(dve_step, 1)
                dve.wait_ge(dve_step, count[0])

            for p in range(2):
                nc.vector.memset(qst[p].rearrange("p h q -> p (h q)"), 0.0).then_inc(const_ready, 1)
                step(nc.vector.memset(kst[p].rearrange("p h n -> p (h n)"), 0.0))
            for p in range(2):
                nc.vector.memset(vp[:, 4 * p:4 * p + 4, :], 1.0).then_inc(const_ready, 1)
            dve.wait_ge(pads_out, 32)
            for p in range(2):
                nc.vector.memset(kst[p][32:64, :, 0:SK], 1.0).then_inc(setup_dve, 1)
                nc.vector.memset(kst[p][96:128, :, SK:2 * SK], 1.0).then_inc(setup_dve, 1)
            dve.wait_ge(smalls_in, 16 * 9)
            for k in range(KC):
                nc.vector.tensor_scalar(pj_sb[:, k, :], pj_sb[:, k, :], normw[:, k:k + 1], None, ALU.mult).then_inc(setup_dve, 1)
            step(nc.vector.tensor_tensor(lams[:, 2, :], lams[:, 1, :], lams[:, 0, :], ALU.subtract))
            step(nc.vector.tensor_scalar(lams[:, 2, :], lams[:, 2, :], -0.1, None, ALU.add))
            for m in range(4):
                dve.wait_ge(kh_ready, 2 * m + 2)
                for n in range(2):
                    w = B * SK // 2
                    c = slice(n * w, (n + 1) * w)
                    ins = nc.vector.scalar_tensor_tensor(out=kl[:, m, c], in0=bank[2 * (m % 2) + n][:, 0:w], scalar=SCALE, in1=kh[:, m, c],
                                                         op0=ALU.mult, op1=ALU.subtract)
                ins.then_inc(kl_ready, 1)
            for b in range(B):
                dve.wait_ge(v_mm, b + 1)
                v = vp[0:SK, b, 0:H * VW].rearrange("p (h d) -> p h d", h=H)[:, :, 0:HD]
                nc.vector.tensor_copy(v, ot_bank[b % 2][0:SK, 0:D].rearrange("p (h d) -> p h d", h=H)).then_inc(v_ready, 1)

            def ln1(b):
                dve.wait_ge(xa_in, 16 * (b + 1))
                for t in range(TPB):
                    if TPB * b > 0:
                        dve.wait_ge(xn_ready, TPB * b)
                    step(nc.vector.bn_stats(bn[:, 0, t, :], xa[:, t, :]))
                    nc.vector.bn_aggr(mv[:, 0, t, :], bn[:, 0, t, :]).then_inc(ln1_stats, 1)
                for t in range(TPB):
                    dve.wait_ge(ln1_rstd, TPB * b + t + 1)
                    if b > 0:
                        dve.wait_ge(xt_mm, b)
                    nc.vector.tensor_scalar(xn[:, t, :], xa[:, t, :], mv[:, 0, t, 0:1], rstd[:, 0, t:t + 1],
                                            ALU.subtract, ALU.mult).then_inc(xn_ready, 1)

            def q_lo(b):
                for a, A in ((0, A6), (1, A7)):
                    dve.wait_ge(qh_ready, 2 * b + a + 1)
                    m = slice(2 * a, 2 * a + 2)
                    nc.vector.tensor_tensor(ql[:, m, :].rearrange("p m n -> p (m n)"), A[:, :], qh[:, m, :].rearrange("p m n -> p (m n)"),
                                            ALU.subtract).then_inc(ql_ready, 1)

            def maxima(b, g):
                t, heads = score_group(g)
                k = len(heads)
                dve.wait_ge(sc_mm, 12 * b + g + 1)
                nc.vector.tensor_reduce(mx[:, t, heads[0]:heads[0] + k, :].rearrange("p h a -> p (h a)"),
                                        sc_bank[g % 2][:, 0:2 * SK * k].rearrange("p (n k) -> p n k", k=SK), AX.X, ALU.max).then_inc(mx_ready, 1)

            def ots_copy(b, g):
                dve.wait_ge(pv_mm, H * b + 4 * g + 4)
                if TPB * b > 0:
                    dve.wait_ge(dt_mm, TPB * b)
                nc.vector.tensor_copy(ots[:, g, :], ot_bank[g % 2][:, :]).then_inc(ots_ready, 1)

            def negate(b):
                dve.wait_ge(mx_ready, 12 * (b + 1))
                if b > 0:
                    dve.wait_ge(mt_mm, b)
                for t in range(TPB):
                    src = mx[:, t].rearrange("p h a -> p a h")
                    step(nc.vector.tensor_scalar(mneg[:, t, 0], src, -1.0, None, ALU.mult))
                    nc.vector.scalar_tensor_tensor(out=mneg[:, t, 1], in0=src, scalar=-1.0, in1=mneg[:, t, 0],
                                                   op0=ALU.mult, op1=ALU.subtract).then_inc(mneg_ready, 1)

            ln1(0)
            q_lo(0)
            for g in range(12):
                maxima(0, g)
            negate(0)
            for b in range(B + 1):
                for h in range(H):
                    if b < B and h % 4 == 0 and h > 0:
                        ots_copy(b, h // 4 - 1)
                    for kind, i, bb in steps(b, h):
                        n = TPB * bb + i
                        if kind == "XT":
                            ln1(bb)
                        if kind == "Q":
                            q_lo(bb)
                        if kind == "SC":
                            maxima(bb, i)
                        if kind == "MT":
                            negate(bb)
                        if kind == "DT":
                            dve.wait_ge(dt_mm, n + 1)
                            u = [A[:, :].rearrange("p (h d) -> p h d", h=H) for A in (A6, A7)]
                            step(nc.vector.reciprocal(rc[:, 0, :], u[0][:, :, HD]))
                            step(nc.vector.reciprocal(rc[:, 1, :], u[1][:, :, HD]))
                            step(nc.vector.tensor_tensor(rc[:, 1, :], rc[:, 1, :], lams[:, 2, :], ALU.mult))
                            if n - 1 > 0:
                                dve.wait_ge(pj_mm, n - 1)
                            for a, dst in ((0, o_sb), (1, o_b)):
                                step(nc.vector.tensor_tensor(dst[:, i, :].rearrange("p (h d) -> p h d", h=H), u[a][:, :, 0:HD],
                                                             rc[:, a, :].unsqueeze(2).broadcast_to([P, H, HD]), ALU.mult))
                            nc.vector.tensor_tensor(o_sb[:, i, :], o_sb[:, i, :], o_b[:, i, :], ALU.add).then_inc(o_ready, 1)
                        if kind == "PJ":
                            dve.wait_ge(pj_mm, n + 1)
                            dve.wait_ge(rms_ready, n + 1)
                            dve.wait_ge(xd_in, 16 * (bb + 1))
                            if 16 * bb > 0:
                                dve.wait_ge(xm_out[i], 16 * bb)
                            nc.vector.scalar_tensor_tensor(out=xmid[:, i, :], in0=A7[:, 0:D], scalar=rstd[:, 2, i:i + 1], in1=xd[:, i, :],
                                                           op0=ALU.mult, op1=ALU.add).then_inc(xm1_ready, 1)
                            dve.wait_ge(xm1_ready, n + 1)
                            nc.vector.tensor_tensor(xmid[:, i, :], xmid[:, i, :], bias_bc, ALU.add).then_inc(xm_ready, 1)
                            dve.wait_ge(xm_ready, n + 1)
                            step(nc.vector.bn_stats(bn[:, 1, i, :], xmid[:, i, :]))
                            nc.vector.bn_aggr(mv[:, 1, i, :], bn[:, 1, i, :]).then_inc(ln2_stats, 1)
                        if kind == "X2":
                            dve.wait_ge(ln2_rstd, n + 1)
                            if n - 1 > 0:
                                dve.wait_ge(x2t_mm, n - 1)
                            nc.vector.tensor_scalar(x2[:, i, :], xmid[:, i, :], mv[:, 1, i, 0:1], rstd[:, 1, i:i + 1],
                                                    ALU.subtract, ALU.mult).then_inc(x2_ready, 1)
                            dve.wait_ge(x2h_ready, n + 1)
                            nc.vector.tensor_tensor(x2s[:, i, 1, :], x2[:, i, :], x2s[:, i, 0, :], ALU.subtract).then_inc(x2l_ready, 1)
                        if kind == "LG":
                            dve.wait_ge(lg_mm, n + 1)
                            nc.vector.tensor_copy(logits[:, n, :], A7[:, 0:E]).then_inc(lg_ready, 1)
                if b < B:
                    ots_copy(b, 3)
            def bc(v, n):
                return v.unsqueeze(2).broadcast_to([P, v.shape[1], n])

            dve.wait_ge(lg_ready, TT)
            dve.wait_ge(rconst_ready, 5)
            prev = logits
            for c, m in ((0, r_m1), (1, r_m2)):
                step(nc.vector.tensor_reduce(m, prev, AX.X, ALU.max))
                if c == 1:
                    nc.vector.tensor_tensor(r_diff, r_m2, r_m1, ALU.subtract).then_inc(route_d, 1)
                step(nc.vector.tensor_tensor(r_eq, prev, bc(m, E), ALU.is_equal))
                step(nc.vector.tensor_tensor(r_key, r_eq, r_rank, ALU.mult))
                step(nc.vector.tensor_reduce(r_top, r_key, AX.X, ALU.max))
                step(nc.vector.tensor_tensor(r_oh[c], r_key, bc(r_top, E), ALU.is_equal))
                if c == 0:
                    step(nc.vector.scalar_tensor_tensor(out=r_two, in0=r_oh[0], scalar=-3.0e38, in1=logits, op0=ALU.mult, op1=ALU.add))
                    prev = r_two
            nc.vector.tensor_tensor(r_mask.rearrange("p e t -> p t e"), r_oh[0], r_oh[1], ALU.add).then_inc(route_m, 1)
            nc.vector.memset(r_one8, 1.0).then_inc(dve_step, 1)
            count[0] += 1
            step(nc.vector.memset(r_reset.rearrange("p e t -> p (e t)"), 1.0))
            step(nc.vector.memset(r_reset[:, :, 0:1], 0.0))
            dve.wait_ge(route_a, 1)
            step(nc.vector.tensor_scalar(r_w[:, 0:TT], r_exp, 1.0, None, ALU.add))
            step(nc.vector.reciprocal(r_w[:, 0:TT], r_w[:, 0:TT]))
            step(nc.vector.tensor_tensor(r_w[:, TT:2 * TT], r_exp, r_w[:, 0:TT], ALU.mult))
            step(nc.vector.tensor_copy(r_wh, r_w))
            step(nc.vector.tensor_tensor(r_wl, r_w, r_wh, ALU.subtract))
            dve.wait_ge(route_mm, 1)
            flat = lambda v: v.rearrange("p e t -> p (e t)")
            step(nc.vector.tensor_copy(flat(r_tot), bank[1][:, 0:P]))
            step(nc.vector.tensor_tensor_scan(flat(r_inc), flat(r_reset), flat(r_tot), 0.0, ALU.mult, ALU.add))
            step(nc.vector.tensor_tensor(flat(r_slot), flat(r_inc), flat(r_tot), ALU.subtract))
            step(nc.vector.tensor_tensor(flat(r_slot), flat(r_slot), bank[0][:, 0:P], ALU.add))
            step(nc.vector.tensor_scalar(r_cnti, r_inc[:, :, TT - 1], float(P - 1), None, ALU.add))
            step(nc.vector.tensor_single_scalar(r_cntj, r_cnti, 7, ALU.arith_shift_right))
            step(nc.vector.tensor_copy(r_nt, r_cntj))
            step(nc.vector.tensor_tensor_scan(r_end, r_one8, r_nt, 0.0, ALU.mult, ALU.add))
            step(nc.vector.tensor_tensor(r_base, r_end, r_nt, ALU.subtract))
            step(nc.vector.tensor_scalar(r_base, r_base, float(P), None, ALU.mult))
            step(nc.vector.tensor_tensor(r_slot, r_slot, bc(r_base, TT), ALU.add))
            for c in range(2):
                step(nc.vector.tensor_tensor(r_key, r_oh[c], r_slot.rearrange("p e t -> p t e"), ALU.mult))
                step(nc.vector.tensor_reduce(r_sl[:, c * TT:(c + 1) * TT], r_key, AX.X, ALU.add))
            step(nc.vector.tensor_copy(r_sli, r_sl))
            step(nc.vector.tensor_single_scalar(r_tilei, r_sli, 7, ALU.arith_shift_right))
            step(nc.vector.tensor_single_scalar(r_posi, r_sli, P - 1, ALU.bitwise_and))
            step(nc.vector.tensor_copy(r_tile, r_tilei))
            step(nc.vector.tensor_copy(r_pos, r_posi))
            J = 2 * TT
            step(nc.vector.tensor_tensor(oneh, r_iota.unsqueeze(1).broadcast_to([P, J, P]), bc(r_pos, P), ALU.is_equal))
            step(nc.vector.tensor_tensor(rtab[:, :, 0, :], r_iota[:, 0:NTP].unsqueeze(1).broadcast_to([P, J, NTP]), bc(r_tile, NTP), ALU.is_equal))
            for c in range(2):
                h = slice(c * TT, (c + 1) * TT)
                step(nc.vector.tensor_tensor(rtab[:, h, 1, :], rtab[:, h, 0, :], bc(r_tok, NTP), ALU.mult))
            step(nc.vector.tensor_tensor(rtab[:, :, 2, :], rtab[:, :, 0, :], bc(r_wh, NTP), ALU.mult))
            nc.vector.tensor_tensor(rtab[:, :, 3, :], rtab[:, :, 0, :], bc(r_wl, NTP), ALU.mult).then_inc(route_t, 1)
            cmp = rcmp.rearrange("p (i e) -> p i e", e=E)
            step(nc.vector.tensor_tensor(cmp, bc(r_iota[:, 0:NTP], E), r_end.unsqueeze(1).broadcast_to([P, NTP, E]), ALU.is_ge))
            step(nc.vector.tensor_reduce(r_exf, cmp, AX.X, ALU.add))
            step(nc.vector.tensor_scalar(tile_exp[:, :], r_exf[0:1, :], float(E - 1), None, ALU.min))
            dve.wait_ge(route_mm, 2)
            step(nc.vector.tensor_copy(r_tab.rearrange("p k n -> p (k n)"), bank[2][:, 0:4 * NTP]))
            step(nc.vector.tensor_scalar(r_free, r_tab[:, 0, :], -1.0, 1.0, ALU.mult, ALU.add))
            step(nc.vector.scalar_tensor_tensor(out=slot_tok[:, :], in0=r_free, scalar=r_pad[:, 0:1], in1=r_tab[:, 1, :], op0=ALU.mult, op1=ALU.add))
            nc.vector.tensor_tensor(slot_w[:, :], r_tab[:, 2, :], r_tab[:, 3, :], ALU.add).then_inc(idx_ready, 1)

            def hidden(k, n):
                dve.wait_ge(sil_ready, k + 1)
                nc.vector.tensor_tensor(sil, sil, bank[2 * n + 1][:, :], ALU.mult).then_inc(h_ready, 1)
                dve.wait_ge(hi_ready, k + 1)
                nc.vector.tensor_tensor(hs[n][:, 1, :], sil, hs[n][:, 0, :], ALU.subtract).then_inc(lo_ready, 1)

            def result(i):
                dve.wait_ge(y_mm, i + 1)
                if not at_start(16 * i):
                    dve.wait_ge(y_out, 16 * i)
                nc.vector.tensor_scalar(y_sb, A7[:, 0:D], slot_w[:, bass.ds(i, 1)], None, ALU.mult).then_inc(y_ready, 1)

            def turn(i, first=False):
                hidden(2 * i, 0)
                hidden(2 * i + 1, 1)
                if not first:
                    result(i - 1)

            turn(0, first=True)
            turn(1)
            turn(2)
            with dve.Fori(1, (NT - 3) // 2) as j:
                turn(2 * j + 1)
                turn(2 * j + 2)
            turn(NT - 2)
            turn(NT - 1)
            result(NT - 1)

        @block.tensor
        def _(pe):
            taken = {6: None, 7: None}

            def bank_for(n, sem_name, value):
                if taken[n]:
                    pe.wait_ge(*taken[n])
                taken[n] = (sem_name, value)
                return bank[n]

            pe.wait_ge(kvw_in, 16 * 2 * KC)
            pe.wait_ge(ctx_in, 16 * KC)
            w = B * SK // 2
            for m in range(4):
                if m - 1 > 0:
                    pe.wait_ge(kl_ready, m - 1)
                for n in range(2):
                    for k in range(KC):
                        ins = nc.tensor.matmul(bank[2 * (m % 2) + n][:, 0:w], wk_sb[:, k, m * P:(m + 1) * P], ctx_sb[:, k, n * w:(n + 1) * w],
                                               start=(k == 0), stop=(k == KC - 1))
                ins.then_inc(kv_mm, 1)
            pe.wait_ge(const_ready, 6)
            for b in range(B):
                if b - 1 > 0:
                    pe.wait_ge(v_ready, b - 1)
                for k in range(KC):
                    ins = nc.tensor.matmul(ot_bank[b % 2][0:SK, 0:D], ctx_sb[:, k, b * SK:(b + 1) * SK], wv_sb[:, k, :],
                                           start=(k == 0), stop=(k == KC - 1))
                ins.then_inc(v_mm, 1)

            def transposed_x(b):
                pe.wait_ge(xn_ready, TPB * (b + 1))
                A = bank_for(6, xnT_ready, b + 1)
                for k in range(KC):
                    for t in range(TPB):
                        ins = nc.tensor.transpose(A[:, k * S + t * P:k * S + (t + 1) * P], xn[:, t, k * P:(k + 1) * P], identf)
                ins.then_inc(xt_mm, 1)

            def queries(b):
                pe.wait_ge(wq_in, 16 * KC)
                pe.wait_ge(xnT_ready, b + 1)
                for a in range(2):
                    A = bank_for(6 + a, ql_ready, 2 * b + a + 1)
                    for half in range(2):
                        m = 2 * a + half
                        for k in range(KC):
                            ins = nc.tensor.matmul(A[:, half * S:(half + 1) * S], wq_sb[:, k, m * P:(m + 1) * P], xnT[:, k, :],
                                                   start=(k == 0), stop=(k == KC - 1))
                    ins.then_inc(q_mm, 1)

            def scores_for_max(b, g):
                t, heads = score_group(g)
                if g == 0:
                    pe.wait_ge(qst_in, 96 * (b + 1))
                    pe.wait_ge(kst_in, 96 * (b + 1))
                    pe.wait_ge(kl_ready, 4)
                if 12 * b + g - 1 > 0:
                    pe.wait_ge(mx_ready, 12 * b + g - 1)
                for n, h in enumerate(heads):
                    ins = nc.tensor.matmul(sc_bank[g % 2][:, 2 * SK * n:2 * SK * (n + 1)], qst[b % 2][:, h, t * P:(t + 1) * P], kst[b % 2][:, h, :],
                                           start=True, stop=True)
                ins.then_inc(sc_mm, 1)

            def transposed_max(b):
                pe.wait_ge(mneg_ready, TPB * (b + 1))
                A = bank_for(6, mT_ready, b + 1)
                for t in range(TPB):
                    ins = nc.tensor.transpose(A[0:64, t * 64:(t + 1) * 64].bitcast(BF16), mneg[:, t].rearrange("p s a h -> p (s a h)"), ident[:, :])
                ins.then_inc(mt_mm, 1)

            def scores(b, h):
                n = H * b + h
                if h == 0:
                    pe.wait_ge(m_in, 64 * (b + 1))
                if n - 1 > 0:
                    pe.wait_ge(p_ready, n - 1)
                for a in range(2):
                    ins = nc.tensor.matmul(st_bank[h % 2][0:SK, a * S:(a + 1) * S], kst[b % 2][:, h, a * SK:(a + 1) * SK], qst[b % 2][:, h, :],
                                           start=True, stop=True)
                ins.then_inc(st_mm, 1)

            def weighted_values(b, h):
                n, g = H * b + h, h // 4
                if n == 0:
                    pe.wait_ge(v_ready, B)
                if h % 4 == 0:
                    if 4 * b + g - 1 > 0:
                        pe.wait_ge(ots_ready, 4 * b + g - 1)
                pe.wait_ge(p_ready, n + 1)
                q = 32 * (h % 4)
                nc.tensor.matmul(ot_bank[g % 2][q:q + 32, :], vp[0:SK, b, h * VW:h * VW + 32], pr[h % 2][0:SK, :],
                                 start=True, stop=True).then_inc(pv_mm, 1)

            def heads_to_tokens(n, i):
                pe.wait_ge(ots_ready, 4 * (n // TPB) + 4)
                for a in range(2):
                    A = bank_for(6 + a, o_ready, n + 1)
                    for g in range(4):
                        c = a * S + i * P
                        ins = nc.tensor.transpose(A[:, g * P:(g + 1) * P], ots[:, g, c:c + P], identf)
                ins.then_inc(dt_mm, 1)

            def turned(src, src_sem, n, done, taken_by):
                pe.wait_ge(src_sem, n + 1)
                A = bank_for(6, taken_by, n + 1)
                for k in range(KC):
                    ins = nc.tensor.transpose(A[:, k * P:(k + 1) * P], src[:, k * P:(k + 1) * P], identf)
                ins.then_inc(done, 1)

            def product(src, src_sem, n, weights, width, done, taken_by):
                pe.wait_ge(src_sem, n + 1)
                A = bank_for(7, taken_by, n + 1)
                for k in range(KC):
                    ins = nc.tensor.matmul(A[:, 0:width], src[:, k * P:(k + 1) * P], weights[:, k, :], start=(k == 0), stop=(k == KC - 1))
                ins.then_inc(done, 1)

            transposed_x(0)
            queries(0)
            pe.wait_ge(setup_dve, 6)
            pe.wait_ge(smalls_in, 16 * 9)
            for g in range(12):
                scores_for_max(0, g)
            transposed_max(0)
            scores(0, 0)
            for b in range(B + 1):
                for h in range(H):
                    if b < B and (b, h) != (B - 1, H - 1):
                        scores(b + (h + 1) // H, (h + 1) % H)
                    for kind, i, bb in steps(b, h):
                        n = TPB * bb + i
                        if kind == "XT":
                            transposed_x(bb)
                        if kind == "Q":
                            queries(bb)
                        if kind == "SC":
                            scores_for_max(bb, i)
                        if kind == "MT":
                            transposed_max(bb)
                        if kind == "DT":
                            heads_to_tokens(n, i)
                        if kind == "OT":
                            turned(o_sb[:, i, :], o_ready, n, otr_mm, oT_ready)
                        if kind == "PJ":
                            product(oT, oT_ready, n, pj_sb, D, pj_mm, xm1_ready)
                        if kind == "X2":
                            turned(x2[:, i, :], x2_ready, n, x2t_mm, x2T_ready)
                        if kind == "LG":
                            product(x2T, x2T_ready, n, gate_sb, E, lg_mm, lg_ready)
                    if b < B:
                        weighted_values(b, h)

            pe.wait_ge(route_m, 1)
            mask = r_mask.rearrange("p e t -> p (e t)")
            nc.tensor.matmul(bank[0][:, 0:P], r_before, mask, start=True, stop=True)
            nc.tensor.matmul(bank[1][:, 0:P], r_ones, mask, start=True, stop=True).then_inc(route_mm, 1)
            pe.wait_ge(route_t, 1)
            for j in range(2 * TT):
                ins = nc.tensor.matmul(bank[2][:, 0:4 * NTP], oneh[:, j, :], rtab[:, j].rearrange("p k n -> p (k n)"),
                                       start=(j == 0), stop=(j == 2 * TT - 1))
            ins.then_inc(route_mm, 1)

            wf = WE[:, :, :].rearrange("p e n -> p (e n)")

            def turned_rows(i, p):
                pe.wait_ge(xg_in[p], 16 * ((i - p) // 2 + 1) if isinstance(i, int) else 8 * (i - p) + 16)
                if not at_start(i):
                    pe.wait_ge(xgT_ready, i)
                A = A6[:, 0:256].bitcast(BF16)
                for c in range(4):
                    ins = nc.tensor.transpose(A[:, c * P:(c + 1) * P], xg[p][:, c * P:(c + 1) * P], ident[:, :])
                ins.then_inc(xgt_mm, 1)

            def up(i, p, n, at):
                k = 2 * i + n
                if n == 0:
                    pe.wait_ge(xgT_ready, i + 1)
                if not at_start(k - 1):
                    pe.wait_ge(sil_ready, k - 1)
                if not at_start(k - 1):
                    pe.wait_ge(h_ready, k - 1)
                terms = [(part, kc, wpart) for kc in range(KC) for part, wparts in ((0, (0, 1)), (1, (0,))) for wpart in wparts]
                for z, (part, kc, wpart) in enumerate(terms):
                    for gu in range(2):
                        o = wpart * W1N + kc * 2 * FF + gu * FF + n * 512
                        ins = nc.tensor.matmul(bank[2 * n + gu][:, :], xgT[p][:, 2 * part + kc, :], wf[:, bass.ds(at + o, 512)],
                                               start=(z == 0), stop=(z == len(terms) - 1))
                ins.then_inc(g_mm, 1)

            def turned_hidden(k, n):
                pe.wait_ge(lo_ready, k + 1)
                if not at_start(k - 1):
                    pe.wait_ge(hT_ready, k - 1)
                A = bank[4 + n][:, :].bitcast(BF16)
                for c in range(8):
                    ins = nc.tensor.transpose(A[:, c * P:(c + 1) * P], hs[n][:, c // 4, (c % 4) * P:(c % 4 + 1) * P], ident[:, :])
                ins.then_inc(ht_mm, 1)

            def down(i, at):
                pe.wait_ge(hT_ready, 2 * i + 2)
                if not at_start(i):
                    pe.wait_ge(y_ready, i)
                terms = [(c, part, wpart) for c in range(FC) for part, wpart in ((0, 0), (0, 1), (1, 0))]
                for z, (c, part, wpart) in enumerate(terms):
                    o = 2 * W1N + wpart * W2N + c * D
                    ins = nc.tensor.matmul(A7[:, 0:D], hT[c // 4][:, 4 * part + c % 4, :], wf[:, bass.ds(at + o, D)],
                                           start=(z == 0), stop=(z == len(terms) - 1))
                ins.then_inc(y_mm, 1)

            def weights_at(i):
                e = pe.value_load(tile_exp[0:1, bass.ds(i, 1)], min_val=0, max_val=E - 1)
                return pe.snap(e * EW)

            def turn(i, p, first=False, last=False):
                at = weights_at(i)
                up(i, p, 0, at)
                if not first:
                    turned_hidden(2 * i - 1, 1)
                up(i, p, 1, at)
                if not first:
                    down(i - 1, weights_at(i - 1))
                turned_hidden(2 * i, 0)
                if not last:
                    turned_rows(i + 1, 1 - p)

            pe.wait_ge(idx_ready, 1)
            pe.wait_ge(w_lo, E * NCH)
            turned_rows(0, 0)
            turn(0, 0, first=True)
            turn(1, 1)
            turn(2, 0)
            with pe.Fori(1, (NT - 3) // 2) as j:
                turn(2 * j + 1, 1)
                turn(2 * j + 2, 0)
            turn(NT - 2, 1)
            turn(NT - 1, 0, last=True)
            turned_hidden(2 * NT - 1, 1)
            down(NT - 1, weights_at(NT - 1))


_SHAPES = {"x": (T, D), "ctxT": (D, B * SK), "wqT": (D, 2 * D), "wkT": (D, 2 * D), "wvT": (D, D), "projT": (D, D),
           "proj_b": (D,), "norm_w": (D, 1), "lam1": (H,), "lam2": (H,), "gateT": (D, E), "w1": (E, P, W1N), "w2": (E, P, W2N)}


def kernel(**inputs):
    import concourse.bacc as _bacc
    from concourse.bass_utils import run_bass_kernel_spmd as _run

    a = {k: np.asarray(v) for k, v in inputs.items()}
    cont = np.ascontiguousarray
    kv1, kv2 = a["L0_xattn_kv1_w"], a["L0_xattn_kv2_w"]
    arrays = {
        "x": a["x"].reshape(T, D),
        "ctxT": a["ctx_1024"].reshape(B * SK, D).T,
        "wqT": np.concatenate([a["L0_xattn_q1_w"].T, a["L0_xattn_q2_w"].T], axis=1),
        "wkT": np.concatenate([kv1[:D].T, kv2[:D].T], axis=1),
        "wvT": kv1[D:].T,
        "projT": a["L0_xattn_proj_w"].T,
        "proj_b": a["L0_xattn_proj_b"],
        "norm_w": a["L0_xattn_norm_w"].reshape(D, 1),
        "lam1": a["L0_xattn_lambda_1"].reshape(H),
        "lam2": a["L0_xattn_lambda_2"].reshape(H),
        "gateT": a["L0_ffn_gate_w"].T,
        "w1": a["L0_ffn_gate_up_proj"].transpose(0, 2, 1).reshape(E, KC, P, 2 * FF).transpose(0, 2, 1, 3).reshape(E, P, W1N),
        "w2": a["L0_ffn_down_proj"].transpose(0, 2, 1).reshape(E, FC, P, D).transpose(0, 2, 1, 3).reshape(E, P, W2N),
    }
    nc = _bacc.Bacc("TRN2", target_bir_lowering=False, num_devices=1)
    args = [nc.dram_tensor(n, shape, F32, kind="ExternalInput").ap() for n, shape in _SHAPES.items()]
    out = nc.dram_tensor("out", (T + P, D), F32, kind="ExternalOutput").ap()
    moe_attention_kernel(nc, *args, out)
    r = _run(nc, [{k: cont(v) for k, v in arrays.items()}], core_ids=[0])
    return r.results[0]["out"][:T].reshape(B, S, D)
```

```python
from contextlib import ExitStack

import numpy as np

import concourse.bass as bass
from concourse import mybir

F32 = mybir.dt.float32
BF16 = mybir.dt.bfloat16
F16 = mybir.dt.float16
I32 = mybir.dt.int32
U32 = mybir.dt.uint32
ALU = mybir.AluOpType
ACT = mybir.ActivationFunctionType
AX = mybir.AxisListType

P = 128
B, S, D = 8, 256, 256
SK = 77
H, HD = 16, 16
E, FF = 8, 1024
T = B * S
TT = T // P
TPB = S // P
KC = D // P
FC = FF // P
NT = (2 * T + E * (P - 1)) // P
NTP = NT
SCALE = HD ** -0.5
VW = HD + 1
W1N, W2N = KC * 2 * FF, FC * D
EW = 2 * (W1N + W2N)
CH = 1024
NCH = (W1N + W2N) // CH
EARLY = 4
STG = 2
ORDER = (0, 1, 2, 3, 5, 6, 4, 7)
CPB = EARLY * NCH // B


def at_start(n):
    return isinstance(n, int) and n <= 0


def moe_attention_kernel(nc, x, ctxT, wqT, wkT, wvT, projT, proj_b, norm_w, lam1, lam2, gateT, w1, w2, out):
    ctx = ExitStack()
    with ctx:
        def sb(name, shape, dt):
            return ctx.enter_context(nc.sbuf_tensor(name, shape, dt))

        def sem(name):
            return ctx.enter_context(nc.semaphore(name))

        WE = sb("WE", [P, E, EW], BF16)
        FB = sb("FB", [P, 15360 // 2], BF16)
        ident = sb("ident", [P, P], BF16)
        slot_tok = sb("slot_tok", [P, NTP], I32)
        slot_w = sb("slot_w", [P, NTP], F32)
        idx_now = sb("idx_now", [P, 3], I32)
        idx_g, idx_s = [idx_now[:, 0:1], idx_now[:, 1:2]], idx_now[:, 2:3]
        pause = sb("pause", [P, 2], BF16)
        tile_exp = sb("tile_exp", [1, NTP], I32)

        def carver(flat, limit):
            at = [0]

            def take(n, dt=F32, parts=P):
                size = n * (2 if dt in (BF16, F16) else 4) // 2
                size += size % 2
                v = flat[0:parts, at[0]:at[0] + size]
                at[0] += size
                assert at[0] <= limit, (at[0], limit)
                return v if dt == BF16 else v.bitcast(dt)
            return take

        late = WE[:, EARLY:E, :].rearrange("p e n -> p (e n)")
        tail = late[:, 3 * EW:4 * EW]
        big = carver(late, 3 * EW)
        att = carver(FB[:, :], 3072)
        setup = carver(tail, EW)

        qst = [big(H * S, BF16).rearrange("p (h q) -> p h q", h=H) for _ in range(2)]
        kst = [big(H * 2 * SK, BF16).rearrange("p (h n) -> p h n", h=H) for _ in range(2)]
        VWP = H * VW + 16
        vp = big(B * VWP).rearrange("p (b n) -> p b n", b=B)
        wq_sb = big(KC * 2 * D).rearrange("p (k n) -> p k n", k=KC)
        pj_sb = big(KC * D).rearrange("p (k n) -> p k n", k=KC)
        ots = big(4 * 512).rearrange("p (g n) -> p g n", g=4)
        pr = [big(512) for _ in range(2)]
        xn = att(TPB * D).rearrange("p (t n) -> p t n", t=TPB)
        xnT = att(KC * S).rearrange("p (k n) -> p k n", k=KC)
        qh = att(4 * S, BF16).rearrange("p (m n) -> p m n", m=4)
        ql = big(4 * S, BF16).rearrange("p (m n) -> p m n", m=4)
        xa = big(TPB * D).rearrange("p (t n) -> p t n", t=TPB)
        xd = big(TPB * D).rearrange("p (t n) -> p t n", t=TPB)
        bias_bc = big(D)
        mT = big(S, BF16)
        o_sb = big(TPB * D).rearrange("p (t n) -> p t n", t=TPB)
        xmid = big(TPB * D).rearrange("p (t n) -> p t n", t=TPB)
        x2 = big(TPB * D).rearrange("p (t n) -> p t n", t=TPB)
        x2s = big(TPB * 2 * D, BF16).rearrange("p (t s n) -> p t s n", t=TPB, s=2)
        identf = big(P)
        gate_sb = big(KC * E).rearrange("p (k n) -> p k n", k=KC)
        mx = big(TPB * 2 * H).rearrange("p (t h a) -> p t h a", t=TPB, a=2)
        mneg = big(TPB * 2 * 2 * H, BF16).rearrange("p (t a s h) -> p t a s h", t=TPB, s=2, a=2)
        bn = big(TPB * 2 * 6).rearrange("p (w t n) -> p w t n", w=2, t=TPB)
        mv = big(TPB * 2 * 2).rearrange("p (w t n) -> p w t n", w=2, t=TPB)
        veps = big(TPB * 3).rearrange("p (w t) -> p w t", w=3)
        rstd = big(TPB * 3).rearrange("p (w t) -> p w t", w=3)
        sumsq = big(TPB)
        rc = big(2 * H).rearrange("p (a h) -> p a h", a=2)
        lams = big(3 * H).rearrange("p (a h) -> p a h", a=3)
        normw = big(KC)
        negh = big(2)
        wk_sb = setup(KC * 2 * D).rearrange("p (k n) -> p k n", k=KC)
        wv_sb = setup(KC * D).rearrange("p (k n) -> p k n", k=KC)
        ctx_sb = setup(KC * B * SK).rearrange("p (k n) -> p k n", k=KC)
        kh = setup(4 * B * SK, BF16).rearrange("p (m n) -> p m n", m=4)
        kl = setup(4 * B * SK, BF16).rearrange("p (m n) -> p m n", m=4)
        after = carver(tail, 2 * KC * 3 * D)
        o_b = after(TPB * D).rearrange("p (t n) -> p t n", t=TPB)
        oT, x2T, sq_junk = after(KC * P), after(KC * P), after(D)

        rt = carver(late, EW)
        oneh = rt(2 * TT * P, F16).rearrange("p (j n) -> p j n", j=2 * TT)
        rtab = rt(2 * TT * 4 * NTP, F16).rearrange("p (j k n) -> p j k n", j=2 * TT, k=4)
        te = lambda v: v.rearrange("p (t e) -> p t e", t=TT)
        et = lambda v: v.rearrange("p (e t) -> p e t", e=E)
        r_eq, r_key, r_two = te(rt(TT * E)), te(rt(TT * E)), te(rt(TT * E))
        r_oh = [te(rt(TT * E)) for _ in range(2)]
        r_tot, r_inc, r_slot, r_reset = (et(rt(TT * E)) for _ in range(4))
        sm = carver(FB[:, :], 3072)
        r_rank = te(sm(TT * E))
        r_iota = sm(P)
        r_tok = sm(TT)
        r_pad = sm(1)
        r_mask = et(sm(TT * E, BF16))
        r_before, r_ones = sm(P, BF16), sm(P, BF16)
        r_m1, r_m2, r_top, r_diff, r_exp = (sm(TT) for _ in range(5))
        r_w = sm(2 * TT)
        r_wh, r_wl = sm(2 * TT, F16), sm(2 * TT, F16)
        r_sl, r_tile, r_pos = sm(2 * TT), sm(2 * TT), sm(2 * TT)
        r_sli, r_tilei, r_posi = sm(2 * TT, I32), sm(2 * TT, I32), sm(2 * TT, I32)
        r_cnt, r_cnti, r_cntj, r_nt, r_end, r_base, r_one8 = sm(E), sm(E, I32), sm(E, I32), sm(E), sm(E), sm(E), sm(E)
        r_tab = sm(4 * NTP).rearrange("p (k n) -> p k n", k=4)
        r_free = sm(NTP)
        r_exf = sm(NTP)
        rcmp = sm(NTP * E)

        ffb = carver(FB[:, :], 7680)
        xg = [ffb(2 * D, BF16) for _ in range(2)]
        xgT = [ffb(2 * D, BF16).rearrange("p (c n) -> p c n", c=4) for _ in range(2)]
        sil = ffb(512)
        hs = [ffb(1024, BF16).rearrange("p (s n) -> p s n", s=2) for _ in range(2)]
        hT = [ffb(1024, BF16).rearrange("p (c n) -> p c n", c=8) for _ in range(2)]
        y_sb = ffb(D)
        stage = [FB[:, 3072 + 2 * CH * n:3072 + 2 * CH * (n + 1)].bitcast(F32) for n in range(STG)]
        stage += [tail[:, 2 * CH * n:2 * CH * (n + 1)].bitcast(F32) for n in range(NCH)]
        stage += [FB[:, 1024:1024 + 2 * CH].bitcast(F32)]
        logits = FB[:, 7168:7168 + 2 * TT * E].bitcast(F32).rearrange("p (t e) -> p t e", t=TT)

        bank = [ctx.enter_context(nc.psum_tensor(f"bank{i}", [P, 512], F32)) for i in range(8)]
        sc_bank, st_bank, ot_bank = bank[0:2], bank[2:4], bank[4:6]
        A6, A7 = bank[6], bank[7]

        QROWS = 3 * HD + 2
        qd = [nc.dram_tensor(f"q_parts{p}", [2, QROWS, H, S], BF16, kind="Internal").ap() for p in range(2)]
        kd = nc.dram_tensor("k_parts", [2, 3 * HD, H, B * SK], BF16, kind="Internal").ap()
        xs = nc.dram_tensor("x_parts", [T + P, 2 * D], BF16, kind="Internal").ap()

        const_ready = sem("const_ready")
        ctx_in = sem("ctx_in")
        kvw_in = sem("kvw_in")
        wq_in = sem("wq_in")
        smalls_in = sem("smalls_in")
        zq_out = sem("zq_out")
        pads_out = sem("pads_out")
        kv_mm = sem("kv_mm")
        kh_ready = sem("kh_ready")
        kl_ready = sem("kl_ready")
        kd_out = sem("kd_out")
        v_mm = sem("v_mm")
        v_ready = sem("v_ready")
        setup_dve = sem("setup_dve")
        xa_in = sem("xa_in")
        ln1_stats = sem("ln1_stats")
        ln1_var = sem("ln1_var")
        ln1_rstd = sem("ln1_rstd")
        xn_ready = sem("xn_ready")
        xt_mm = sem("xt_mm")
        xnT_ready = sem("xnT_ready")
        q_mm = sem("q_mm")
        qh_ready = sem("qh_ready")
        ql_ready = sem("ql_ready")
        qd_out = sem("qd_out")
        sc_mm = sem("sc_mm")
        mx_ready = sem("mx_ready")
        mneg_ready = sem("mneg_ready")
        mt_mm = sem("mt_mm")
        mT_ready = sem("mT_ready")
        m_in = sem("m_in")
        st_mm = sem("st_mm")
        p_ready = sem("p_ready")
        pv_mm = sem("pv_mm")
        ots_ready = sem("ots_ready")
        dt_mm = sem("dt_mm")
        o_ready = sem("o_ready")
        ss_ready = sem("ss_ready")
        rms_var = sem("rms_var")
        rms_ready = sem("rms_ready")
        otr_mm = sem("otr_mm")
        oT_ready = sem("oT_ready")
        pj_mm = sem("pj_mm")
        xd_in = sem("xd_in")
        xm1_ready = sem("xm1_ready")
        xm_ready = sem("xm_ready")
        ln2_stats = sem("ln2_stats")
        ln2_var = sem("ln2_var")
        ln2_rstd = sem("ln2_rstd")
        x2_ready = sem("x2_ready")
        x2h_ready = sem("x2h_ready")
        x2l_ready = sem("x2l_ready")
        x2t_mm = sem("x2t_mm")
        x2T_ready = sem("x2T_ready")
        lg_mm = sem("lg_mm")
        lg_ready = sem("lg_ready")
        w_hi = sem("w_hi")
        w_lo = sem("w_lo")
        w_lo_dve = sem("w_lo_dve")
        route_d = sem("route_d")
        route_a = sem("route_a")
        route_m = sem("route_m")
        route_t = sem("route_t")
        route_mm = sem("route_mm")
        idx_ready = sem("idx_ready")
        idxg_ready = sem("idxg_ready")
        idxs_ready = sem("idxs_ready")
        rconst_ready = sem("rconst_ready")
        xgt_mm = sem("xgt_mm")
        xgT_ready = sem("xgT_ready")
        g_mm = sem("g_mm")
        sil_ready = sem("sil_ready")
        h_ready = sem("h_ready")
        hi_ready = sem("hi_ready")
        lo_ready = sem("lo_ready")
        ht_mm = sem("ht_mm")
        hT_ready = sem("hT_ready")
        y_mm = sem("y_mm")
        y_ready = sem("y_ready")
        y_out = sem("y_out")
        dve_step = sem("dve_step")
        pool_step = sem("pool_step")
        kst_in = [sem(f"kst_in{p}") for p in range(2)]
        qst_in = [sem(f"qst_in{p}") for p in range(2)]
        xm_out = [sem(f"xm_out{p}") for p in range(2)]
        x2_out = [sem(f"x2_out{p}") for p in range(2)]
        stage_in = [sem(f"stage_in{p}") for p in range(STG + NCH + 1)]
        xg_in = [sem(f"xg_in{p}") for p in range(2)]

        block = ctx.enter_context(nc.Block())

        STEPS = {1: [("DT", 0)], 2: [("LS", 0)], 3: [("SC", 0), ("SC", 1), ("OT", 0)],
                 4: [("SC", 2), ("SC", 3), ("PJ", 0), ("LN", 0)], 5: [("DT", 1)], 6: [("XT", 0), ("SC", 4), ("SC", 5)],
                 7: [("SC", 6), ("SC", 7), ("OT", 1)], 8: [("SC", 8), ("SC", 9), ("PJ", 1)],
                 9: [("Q", 0), ("SC", 10), ("SC", 11)], 10: [("X2", 0), ("MT", 0)], 11: [("LG", 0)],
                 12: [("X2", 1)], 13: [("LG", 1)], 15: [("QI", 0)]}
        WSTEP = {1: 0, 6: 1, 11: 2}
        OTS = {6: 0, 9: 1, 13: 2}
        AHEAD = {"LS": 2, "LN": 2, "XT": 2, "Q": 2, "QI": 2, "SC": 1, "MT": 1}

        def steps(b, h):
            for kind, i in STEPS.get(h, []):
                bb = b + AHEAD.get(kind, -1)
                if 0 <= bb < B and (bb >= AHEAD.get(kind, 0)):
                    yield kind, i, bb

        def score_group(g):
            t, u = g // 6, g % 6
            return t, range(3 * u, min(3 * u + 3, H))

        def piece(n):
            e, c = ORDER[n // NCH], n % NCH
            if c < W1N // CH:
                return w1[e, :, c * CH:(c + 1) * CH], WE[:, e, c * CH:(c + 1) * CH], WE[:, e, W1N + c * CH:W1N + (c + 1) * CH]
            c -= W1N // CH
            o = 2 * W1N + c * CH
            return w2[e, :, c * CH:(c + 1) * CH], WE[:, e, o:o + CH], WE[:, e, o + W2N:o + W2N + CH]

        def place(n):
            n -= EARLY * NCH
            if n < STG:
                return n % STG
            if n < 3 * NCH:
                return (n - STG) % (STG + NCH) + STG if (n - STG) % (STG + NCH) < NCH else (n - STG) % (STG + NCH) - NCH
            return (STG + NCH, 0, 1)[n % 3]

        def uses(n):
            return sum(place(m) == place(n) for m in range(n + 1))

        def before(n):
            return max((m for m in range(n) if place(m) == place(n)), default=None)

        def on_dve(n):
            return n >= (EARLY + 2) * NCH and n % 3 != 0

        def lows(n, dve):
            return sum(on_dve(m) == dve for m in range(n + 1))

        @block.sync
        def _(sp):
            def load_x(b):
                if 2 * b > 0:
                    sp.wait_ge(xn_ready, 2 * b)
                sp.dma_start(xa, x[b * S:(b + 1) * S, :].rearrange("(t p) n -> p t n", p=P)).then_inc(xa_in, 16)

            load_x(0)
            for k in range(KC):
                sp.dma_start(wk_sb[:, k, :], wkT[k * P:(k + 1) * P, :]).then_inc(kvw_in, 16)
                sp.dma_start(ctx_sb[:, k, :], ctxT[k * P:(k + 1) * P, :]).then_inc(ctx_in, 16)
                sp.dma_start(wv_sb[:, k, :], wvT[k * P:(k + 1) * P, :]).then_inc(kvw_in, 16)
            for k in range(KC):
                sp.dma_start(wq_sb[:, k, :], wqT[k * P:(k + 1) * P, :]).then_inc(wq_in, 16)
                sp.dma_start(pj_sb[:, k, :], projT[k * P:(k + 1) * P, :]).then_inc(smalls_in, 16)
                sp.dma_start(gate_sb[:, k, :], gateT[k * P:(k + 1) * P, :]).then_inc(smalls_in, 16)
                sp.dma_start(normw[:, k:k + 1], norm_w[k * P:(k + 1) * P, :]).then_inc(smalls_in, 16)
            load_x(1)
            sp.dma_start(bias_bc, proj_b.partition_broadcast(P)).then_inc(smalls_in, 16)
            sp.dma_start(lams[:, 0, :], lam1.partition_broadcast(P)).then_inc(smalls_in, 16)
            sp.dma_start(lams[:, 1, :], lam2.partition_broadcast(P)).then_inc(smalls_in, 16)

            def load_piece(n):
                m = before(n)
                if m is None:
                    if place(n) == STG + NCH:
                        sp.wait_ge(idx_ready, 1)
                elif on_dve(m):
                    sp.wait_ge(w_lo_dve, lows(m, True))
                else:
                    sp.wait_ge(w_lo, lows(m, False))
                sp.dma_start(stage[place(n)], piece(n)[0]).then_inc(stage_in[place(n)], 16)

            for n in range(STG):
                load_piece(n)
            sp.wait_ge(const_ready, 6)
            zrow = kst[0].rearrange("p h n -> p (h n)")
            sp.dma_start(xs[T:T + P, :], zrow[:, 0:2 * D]).then_inc(pads_out, 16)
            sp.dma_start(out[T:T + P, :], zrow[:, 0:2 * D].bitcast(F32)).then_inc(pads_out, 16)
            for p in range(2):
                for a in range(2):
                    sp.dma_start(qd[p][a, 3 * HD:QROWS, :, :].rearrange("r h q -> r (h q)"),
                                 qst[0][0:2].rearrange("p h q -> p (h q)")).then_inc(zq_out, 16)
            def stack_out(dst, r, parts, a, done):
                rows = dst[a, r * HD:(r + 1) * HD].rearrange("d (j half) n -> j d (half n)", half=2)
                src = parts[:, 2 * a:2 * a + 2, :].rearrange("p m n -> p (m n)")
                sp.dma_start(rows, src).then_inc(done, 16)

            sp.wait_ge(kl_ready, 4)
            for a in range(2):
                for r, part in ((0, kh), (1, kl), (2, kh)):
                    stack_out(kd, r, part, a, kd_out)

            def load_k(b):
                if b >= 2:
                    sp.wait_ge(st_mm, H * (b - 1))
                for a in range(2):
                    sp.dma_start(kst[b % 2][64 * a:64 * a + 3 * HD, :, a * SK:(a + 1) * SK],
                                 kd[a, :, :, b * SK:(b + 1) * SK]).then_inc(kst_in[b % 2], 16)

            def queries_out(b):
                if b >= 2:
                    sp.wait_ge(qst_in[b % 2], 32 * (b // 2))
                for a in range(2):
                    sp.wait_ge(qh_ready, 2 * b + a + 1)
                    stack_out(qd[b % 2], 0, qh, a, qd_out)
                    stack_out(qd[b % 2], 1, qh, a, qd_out)
                    sp.wait_ge(ql_ready, 2 * b + a + 1)
                    stack_out(qd[b % 2], 2, ql, a, qd_out)

            def queries_in(b):
                load_k(b)
                sp.wait_ge(qd_out, 96 * (b + 1))
                for a in range(2):
                    sp.dma_start(qst[b % 2][64 * a:64 * a + QROWS, :, :], qd[b % 2][a]).then_inc(qst_in[b % 2], 16)

            def shifts(b):
                sp.wait_ge(mT_ready, b + 1)
                for a in range(2):
                    sp.dma_start(qst[b % 2][64 * a + 48:64 * a + 50, :, :], mT[2 * H * a:2 * H * (a + 1), :]).then_inc(m_in, 16)

            queries_out(0)
            sp.wait_ge(kd_out, 16 * 6)
            sp.wait_ge(setup_dve, 4)
            sp.wait_ge(zq_out, 64)
            queries_in(0)
            queries_out(1)
            queries_in(1)
            load_x(2)
            shifts(0)
            for b in range(B + 1):
                for h in range(H):
                    for kind, i, bb in steps(b, h):
                        if kind == "QI":
                            queries_in(bb)
                        if kind == "Q":
                            queries_out(bb)
                            if bb + 1 < B:
                                load_x(bb + 1)
                        if kind == "MT":
                            shifts(bb)
                        if kind == "DT" and i == 0:
                            if bb >= 1:
                                if 2 * bb > 0:
                                    sp.wait_ge(xm1_ready, 2 * bb)
                            sp.dma_start(xd, x[bb * S:(bb + 1) * S, :].rearrange("(t p) n -> p t n", p=P)).then_inc(xd_in, 16)
                        if kind == "X2":
                            r = bb * S + i * P
                            sp.wait_ge(xm_ready, 2 * bb + i + 1)
                            sp.dma_start(out[r:r + P, :], xmid[:, i, :]).then_inc(xm_out[i], 16)
                        if kind == "LG":
                            r = bb * S + i * P
                            sp.wait_ge(x2l_ready, 2 * bb + i + 1)
                            sp.dma_start(xs[r:r + P, :], x2s[:, i].rearrange("p s n -> p (s n)")).then_inc(x2_out[i], 16)
                    if b < B and h - 1 in WSTEP:
                        load_piece(CPB * b + WSTEP[h - 1] + STG)
            sp.wait_ge(lg_ready, TT)
            for i in range(TPB):
                sp.wait_ge(xm_out[i], 16 * B)
                sp.wait_ge(x2_out[i], 16 * B)
            for n in range(EARLY * NCH + STG, E * NCH):
                load_piece(n)

        @block.gpsimd
        def _(pool):
            pool_count = [0]

            def step(ins, n=pool_count):
                ins.then_inc(pool_step, 1)
                n[0] += 1
                pool.wait_ge(pool_step, n[0])

            step(nc.gpsimd.memset(identf, 0.0))
            step(nc.gpsimd.affine_select(out=identf, in_=identf, compare_op=ALU.not_equal, fill=1.0, base=0,
                                         pattern=[[-1, P]], channel_multiplier=1))
            nc.gpsimd.tensor_copy(ident[:, :], identf).then_inc(const_ready, 1)
            nc.gpsimd.memset(negh, -0.5).then_inc(const_ready, 1)

            def lo_part(n):
                _, hi, lo = piece(n)
                pool.wait_ge(w_hi, n + 1)
                nc.gpsimd.tensor_tensor(lo, stage[place(n)], hi, ALU.subtract).then_inc(w_lo, 1)

            def power(w, t0, n, src, src_sem, count, mul, var_sem, done):
                pool.wait_ge(src_sem, count)
                eps = 1e-6 if w == 2 else 1e-5
                nc.gpsimd.tensor_scalar(veps[:, w, t0:t0 + n], src, mul, eps, ALU.mult, ALU.add).then_inc(var_sem, 1)
                return eps

            step(nc.gpsimd.memset(pause[:, :], 0.0))

            def rsqrt(w, t, src, src_sem, var_sem, done, k):
                power(w, t, 1, src, src_sem, k + 1, 1.0 / D if w == 2 else 1.0, var_sem, done)
                pool.wait_ge(var_sem, k + 1)
                nc.gpsimd.tensor_tensor(rstd[:, w, t:t + 1], veps[:, w, t:t + 1], negh[:, 0:1], ALU.pow).then_inc(done, 1)

            def ln1(b):
                for t in range(TPB):
                    rsqrt(0, t, mv[:, 0, t, 1:2], ln1_stats, ln1_var, ln1_rstd, TPB * b + t)

            ln1(0)
            ln1(1)
            for b in range(B + 1):
                for h in range(H):
                    for kind, i, bb in steps(b, h):
                        if kind == "LS":
                            ln1(bb)
                        if kind == "OT":
                            rsqrt(2, i, sumsq[:, i:i + 1], ss_ready, rms_var, rms_ready, TPB * bb + i)
                        if kind == "PJ":
                            rsqrt(1, i, mv[:, 1, i, 1:2], ln2_stats, ln2_var, ln2_rstd, TPB * bb + i)
                    if b < B and h in WSTEP:
                        lo_part(CPB * b + WSTEP[h])
            pool.wait_ge(lg_ready, TT)
            nc.gpsimd.iota(r_rank, [[0, TT], [-1, E]], base=E, channel_multiplier=0, allow_small_or_imprecise_dtypes=True).then_inc(rconst_ready, 1)
            nc.gpsimd.iota(r_iota, [[1, P]], base=0, channel_multiplier=0, allow_small_or_imprecise_dtypes=True).then_inc(rconst_ready, 1)
            nc.gpsimd.iota(r_tok, [[P, TT]], base=0, channel_multiplier=1, allow_small_or_imprecise_dtypes=True).then_inc(rconst_ready, 1)
            nc.gpsimd.iota(r_pad, [[0, 1]], base=T, channel_multiplier=1, allow_small_or_imprecise_dtypes=True).then_inc(rconst_ready, 1)
            step(nc.gpsimd.memset(r_ones, 1.0), pool_count)
            nc.gpsimd.affine_select(out=r_before, in_=r_ones, compare_op=ALU.is_gt, fill=0.0, base=0,
                                    pattern=[[1, P]], channel_multiplier=-1).then_inc(rconst_ready, 1)
            for n in range(EARLY * NCH, (EARLY + 2) * NCH):
                lo_part(n)

            pool.wait_ge(idx_ready, 1)

            def gather(i, p):
                if not isinstance(i, int) or i >= 2:
                    if not at_start(i - 1):
                        pool.wait_ge(xgt_mm, i - 1)
                nc.gpsimd.tensor_copy(idx_g[p][:, :], slot_tok[:, bass.ds(i, 1)]).then_inc(idxg_ready, 1)
                pool.wait_ge(idxg_ready, i + 1)
                nc.gpsimd.tensor_tensor(pause[:, 0:1], pause[:, 1:2], pause[:, 1:2], ALU.add)
                pool.indirect_dma_start(out=xg[p], out_offset=None, in_=xs,
                                        in_offset=bass.IndirectOffsetOnAxis(ap=idx_g[p][:, 0:1].bitcast(U32), axis=0),
                                        ).then_inc(xg_in[p], 16)

            def scatter(i, p):
                pool.wait_ge(y_ready, i + 1)
                if not at_start(16 * i):
                    pool.wait_ge(y_out, 16 * i)
                nc.gpsimd.tensor_copy(idx_s[:, :], slot_tok[:, bass.ds(i, 1)]).then_inc(idxs_ready, 1)
                pool.wait_ge(idxs_ready, i + 1)
                nc.gpsimd.tensor_tensor(pause[:, 0:1], pause[:, 1:2], pause[:, 1:2], ALU.add)
                pool.indirect_dma_start(out=out, out_offset=bass.IndirectOffsetOnAxis(ap=idx_s[:, 0:1].bitcast(U32), axis=0),
                                        in_=y_sb, in_offset=None, compute_op=ALU.add).then_inc(y_out, 16)

            def turn(i, p, more=True):
                if more:
                    gather(i + 3, 1 - p)
                scatter(i, p)

            gather(0, 0)
            gather(1, 1)
            for n in range((EARLY + 2) * NCH, E * NCH):
                if not on_dve(n):
                    lo_part(n)
            gather(2, 0)
            turn(0, 0)
            turn(1, 1)
            turn(2, 0)
            with pool.Fori(1, (NT - 5) // 2) as j:
                turn(2 * j + 1, 1)
                turn(2 * j + 2, 0)
            turn(NT - 4, 1)
            turn(NT - 3, 0, False)
            turn(NT - 2, 1, False)
            turn(NT - 1, 0, False)
            pool.wait_ge(y_out, 16 * NT)

        @block.scalar
        def _(act):
            for m in range(4):
                act.wait_ge(kv_mm, m + 1)
                for n in range(2):
                    w = B * SK // 2
                    nc.scalar.activation(kh[:, m, n * w:(n + 1) * w], bank[2 * (m % 2) + n][:, 0:w], ACT.Copy, scale=SCALE).then_inc(kh_ready, 1)

            def hi_part(n):
                act.wait_ge(stage_in[place(n)], 16 * uses(n))
                nc.scalar.activation(piece(n)[1], stage[place(n)], ACT.Copy).then_inc(w_hi, 1)

            def xnT_copy(b):
                act.wait_ge(xt_mm, b + 1)
                if 2 * b > 0:
                    act.wait_ge(q_mm, 2 * b)
                nc.scalar.activation(xnT.rearrange("p k n -> p (k n)"), A6[:, :], ACT.Copy).then_inc(xnT_ready, 1)

            def q_hi(b):
                for a, A in ((0, A6), (1, A7)):
                    act.wait_ge(q_mm, 2 * b + a + 1)
                    if 96 * b > 0:
                        act.wait_ge(qd_out, 96 * b)
                    nc.scalar.activation(qh[:, 2 * a:2 * a + 2, :].rearrange("p m n -> p (m n)"), A[:, :], ACT.Copy).then_inc(qh_ready, 1)

            def mt_copy(b):
                act.wait_ge(mt_mm, b + 1)
                if 32 * b > 0:
                    act.wait_ge(m_in, 32 * b)
                nc.scalar.activation(mT[0:64, :], A6[0:64, 0:S // 2].bitcast(BF16), ACT.Copy).then_inc(mT_ready, 1)

            def exp(b, h):
                n = b * H + h
                act.wait_ge(st_mm, n + 1)
                if n - 1 > 0:
                    act.wait_ge(pv_mm, n - 1)
                nc.scalar.activation(pr[h % 2][0:SK, :], st_bank[h % 2][0:SK, :], ACT.Exp).then_inc(p_ready, 1)

            xnT_copy(0)
            q_hi(0)
            xnT_copy(1)
            q_hi(1)
            mt_copy(0)
            exp(0, 0)
            for b in range(B + 1):
                for h in range(H):
                    if b < B and (b, h) != (B - 1, H - 1):
                        exp(b + (h + 1) // H, (h + 1) % H)
                    for kind, i, bb in steps(b, h):
                        n = TPB * bb + i
                        if kind == "XT":
                            xnT_copy(bb)
                        if kind == "Q":
                            q_hi(bb)
                        if kind == "MT":
                            mt_copy(bb)
                        if kind == "OT":
                            act.wait_ge(o_ready, n + 1)
                            nc.scalar.activation(sq_junk, o_sb[:, i, :], ACT.Square, accum_out=sumsq[:, i:i + 1]).then_inc(ss_ready, 1)
                            act.wait_ge(otr_mm, n + 1)
                            if n > 0:
                                act.wait_ge(pj_mm, n)
                            nc.scalar.activation(oT, A6[:, 0:KC * P], ACT.Copy).then_inc(oT_ready, 1)
                        if kind == "X2":
                            act.wait_ge(x2_ready, n + 1)
                            if 16 * bb > 0:
                                act.wait_ge(x2_out[i], 16 * bb)
                            nc.scalar.activation(x2s[:, i, 0, :], x2[:, i, :], ACT.Copy).then_inc(x2h_ready, 1)
                            act.wait_ge(x2t_mm, n + 1)
                            if n > 0:
                                act.wait_ge(lg_mm, n)
                            nc.scalar.activation(x2T, A6[:, 0:KC * P], ACT.Copy).then_inc(x2T_ready, 1)
                    if b < B and h in WSTEP:
                        hi_part(CPB * b + WSTEP[h])
            act.wait_ge(route_d, 1)
            nc.scalar.activation(r_exp, r_diff, ACT.Exp).then_inc(route_a, 1)
            for n in range(EARLY * NCH, E * NCH):
                if n == EARLY * NCH:
                    for i in range(TPB):
                        act.wait_ge(xm_out[i], 16 * B)
                        act.wait_ge(x2_out[i], 16 * B)
                if n == (E - 2) * NCH:
                    act.wait_ge(idx_ready, 1)
                if n == (E - 1) * NCH:
                    act.wait_ge(w_lo_dve, lows(n - 1, True))
                    act.wait_ge(w_lo, lows(n - 1, False))
                hi_part(n)

            def xgT_copy(i, p):
                act.wait_ge(xgt_mm, i + 1)
                nc.scalar.activation(xgT[p].rearrange("p c n -> p (c n)"), A6[:, 0:256].bitcast(BF16), ACT.Copy).then_inc(xgT_ready, 1)

            def hT_copy(k, n):
                act.wait_ge(ht_mm, k + 1)
                nc.scalar.activation(hT[n].rearrange("p c n -> p (c n)"), bank[4 + n][:, :].bitcast(BF16), ACT.Copy).then_inc(hT_ready, 1)

            def gate(k, n):
                act.wait_ge(g_mm, k + 1)
                if not at_start(k):
                    act.wait_ge(lo_ready, k)
                nc.scalar.activation(sil, bank[2 * n][:, :], ACT.Silu).then_inc(sil_ready, 1)
                act.wait_ge(h_ready, k + 1)
                if not at_start(k - 1):
                    act.wait_ge(ht_mm, k - 1)
                nc.scalar.activation(hs[n][:, 0, :], sil, ACT.Copy).then_inc(hi_ready, 1)

            def turn(i, p, first=False, last=False):
                gate(2 * i, 0)
                if not first:
                    hT_copy(2 * i - 1, 1)
                if not last:
                    xgT_copy(i + 1, 1 - p)
                gate(2 * i + 1, 1)
                hT_copy(2 * i, 0)

            act.wait_ge(w_lo_dve, lows(E * NCH - 1, True))
            act.wait_ge(w_lo, lows(E * NCH - 1, False))
            xgT_copy(0, 0)
            turn(0, 0, first=True)
            turn(1, 1)
            turn(2, 0)
            with act.Fori(1, (NT - 3) // 2) as j:
                turn(2 * j + 1, 1)
                turn(2 * j + 2, 0)
            turn(NT - 2, 1)
            turn(NT - 1, 0, last=True)
            hT_copy(2 * NT - 1, 1)

        @block.vector
        def _(dve):
            count = [0]

            def step(ins):
                count[0] += 1
                ins.then_inc(dve_step, 1)
                dve.wait_ge(dve_step, count[0])

            def ln1_stats_of(b):
                dve.wait_ge(xa_in, 16 * (b + 1))
                for t in range(TPB):
                    if b > 0:
                        dve.wait_ge(xn_ready, TPB * b)
                    step(nc.vector.bn_stats(bn[:, 0, t, :], xa[:, t, :]))
                    nc.vector.bn_aggr(mv[:, 0, t, :], bn[:, 0, t, :]).then_inc(ln1_stats, 1)

            def ln1_norm(b):
                for t in range(TPB):
                    dve.wait_ge(ln1_rstd, TPB * b + t + 1)
                    if b > 0:
                        dve.wait_ge(xt_mm, b)
                    nc.vector.tensor_scalar(xn[:, t, :], xa[:, t, :], mv[:, 0, t, 0:1], rstd[:, 0, t:t + 1],
                                            ALU.subtract, ALU.mult).then_inc(xn_ready, 1)

            for p in range(2):
                step(nc.vector.memset(kst[p].rearrange("p h n -> p (h n)").bitcast(F32), 0.0))
                nc.vector.memset(qst[p].rearrange("p h q -> p (h q)").bitcast(F32), 0.0).then_inc(const_ready, 1)
            nc.vector.memset(vp[:, :, 0:H * VW].rearrange("p b (h d) -> p b h d", h=H)[:, :, :, HD], 1.0).then_inc(const_ready, 1)
            nc.vector.memset(vp[:, :, H * VW:VWP], 1.0).then_inc(const_ready, 1)
            ln1_stats_of(0)
            ln1_norm(0)
            dve.wait_ge(pads_out, 32)
            for p in range(2):
                nc.vector.memset(kst[p][32:64, :, 0:SK], 1.0).then_inc(setup_dve, 1)
                nc.vector.memset(kst[p][96:128, :, SK:2 * SK], 1.0).then_inc(setup_dve, 1)
            dve.wait_ge(smalls_in, 16 * 9)
            for k in range(KC):
                nc.vector.tensor_scalar(pj_sb[:, k, :], pj_sb[:, k, :], normw[:, k:k + 1], None, ALU.mult).then_inc(setup_dve, 1)
            step(nc.vector.tensor_tensor(lams[:, 2, :], lams[:, 1, :], lams[:, 0, :], ALU.subtract))
            step(nc.vector.tensor_scalar(lams[:, 2, :], lams[:, 2, :], -0.1, None, ALU.add))
            for m in range(4):
                dve.wait_ge(kh_ready, 2 * m + 2)
                for n in range(2):
                    w = B * SK // 2
                    c = slice(n * w, (n + 1) * w)
                    ins = nc.vector.scalar_tensor_tensor(out=kl[:, m, c], in0=bank[2 * (m % 2) + n][:, 0:w], scalar=SCALE, in1=kh[:, m, c],
                                                         op0=ALU.mult, op1=ALU.subtract)
                ins.then_inc(kl_ready, 1)
            def q_lo(b):
                for a, A in ((0, A6), (1, A7)):
                    dve.wait_ge(qh_ready, 2 * b + a + 1)
                    m = slice(2 * a, 2 * a + 2)
                    nc.vector.tensor_tensor(ql[:, m, :].rearrange("p m n -> p (m n)"), A[:, :], qh[:, m, :].rearrange("p m n -> p (m n)"),
                                            ALU.subtract).then_inc(ql_ready, 1)

            def maxima(b, g):
                t, heads = score_group(g)
                k = len(heads)
                dve.wait_ge(sc_mm, 12 * b + g + 1)
                nc.vector.tensor_reduce(mx[:, t, heads[0]:heads[0] + k, :].rearrange("p h a -> p (h a)"),
                                        sc_bank[g % 2][:, 0:2 * SK * k].rearrange("p (n k) -> p n k", k=SK), AX.X, ALU.max).then_inc(mx_ready, 1)

            def ots_copy(b, g):
                dve.wait_ge(pv_mm, H * b + 4 * g + 4)
                if TPB * b > 0:
                    dve.wait_ge(dt_mm, TPB * b)
                nc.vector.tensor_copy(ots[:, g, :], ot_bank[g % 2][:, :]).then_inc(ots_ready, 1)

            def negate(b):
                dve.wait_ge(mx_ready, 12 * (b + 1))
                if b > 0:
                    dve.wait_ge(mt_mm, b)
                for t in range(TPB):
                    src = mx[:, t].rearrange("p h a -> p a h")
                    step(nc.vector.tensor_scalar(mneg[:, t, :, 0], src, -1.0, None, ALU.mult))
                    nc.vector.scalar_tensor_tensor(out=mneg[:, t, :, 1], in0=src, scalar=-1.0, in1=mneg[:, t, :, 0],
                                                   op0=ALU.mult, op1=ALU.subtract).then_inc(mneg_ready, 1)

            q_lo(0)
            for b in range(B):
                dve.wait_ge(v_mm, b + 1)
                v = vp[0:SK, b, 0:H * VW].rearrange("p (h d) -> p h d", h=H)[:, :, 0:HD]
                nc.vector.tensor_copy(v, ot_bank[b % 2][0:SK, 0:D].rearrange("p (h d) -> p h d", h=H)).then_inc(v_ready, 1)
            ln1_stats_of(1)
            ln1_norm(1)
            q_lo(1)
            for g in range(12):
                maxima(0, g)
            negate(0)
            for b in range(B + 1):
                for h in range(H):
                    if b < B and h in OTS:
                        ots_copy(b, OTS[h])
                    for kind, i, bb in steps(b, h):
                        n = TPB * bb + i
                        if kind == "LS":
                            ln1_stats_of(bb)
                        if kind == "LN":
                            ln1_norm(bb)
                        if kind == "Q":
                            q_lo(bb)
                        if kind == "SC":
                            maxima(bb, i)
                        if kind == "MT":
                            negate(bb)
                        if kind == "DT":
                            dve.wait_ge(dt_mm, n + 1)
                            u = [A[:, :].rearrange("p (h d) -> p h d", h=H) for A in (A6, A7)]
                            step(nc.vector.reciprocal(rc[:, 0, :], u[0][:, :, HD]))
                            step(nc.vector.reciprocal(rc[:, 1, :], u[1][:, :, HD]))
                            step(nc.vector.tensor_tensor(rc[:, 1, :], rc[:, 1, :], lams[:, 2, :], ALU.mult))
                            if n - 1 > 0:
                                dve.wait_ge(pj_mm, n - 1)
                            for a, dst in ((0, o_sb), (1, o_b)):
                                step(nc.vector.tensor_tensor(dst[:, i, :].rearrange("p (h d) -> p h d", h=H), u[a][:, :, 0:HD],
                                                             rc[:, a, :].unsqueeze(2).broadcast_to([P, H, HD]), ALU.mult))
                            nc.vector.tensor_tensor(o_sb[:, i, :], o_sb[:, i, :], o_b[:, i, :], ALU.add).then_inc(o_ready, 1)
                        if kind == "PJ":
                            dve.wait_ge(pj_mm, n + 1)
                            dve.wait_ge(rms_ready, n + 1)
                            dve.wait_ge(xd_in, 16 * (bb + 1))
                            if 16 * bb > 0:
                                dve.wait_ge(xm_out[i], 16 * bb)
                            nc.vector.scalar_tensor_tensor(out=xmid[:, i, :], in0=A7[:, 0:D], scalar=rstd[:, 2, i:i + 1], in1=xd[:, i, :],
                                                           op0=ALU.mult, op1=ALU.add).then_inc(xm1_ready, 1)
                            dve.wait_ge(xm1_ready, n + 1)
                            nc.vector.tensor_tensor(xmid[:, i, :], xmid[:, i, :], bias_bc, ALU.add).then_inc(xm_ready, 1)
                            dve.wait_ge(xm_ready, n + 1)
                            step(nc.vector.bn_stats(bn[:, 1, i, :], xmid[:, i, :]))
                            nc.vector.bn_aggr(mv[:, 1, i, :], bn[:, 1, i, :]).then_inc(ln2_stats, 1)
                        if kind == "X2":
                            dve.wait_ge(ln2_rstd, n + 1)
                            if n - 1 > 0:
                                dve.wait_ge(x2t_mm, n - 1)
                            nc.vector.tensor_scalar(x2[:, i, :], xmid[:, i, :], mv[:, 1, i, 0:1], rstd[:, 1, i:i + 1],
                                                    ALU.subtract, ALU.mult).then_inc(x2_ready, 1)
                            dve.wait_ge(x2h_ready, n + 1)
                            nc.vector.tensor_tensor(x2s[:, i, 1, :], x2[:, i, :], x2s[:, i, 0, :], ALU.subtract).then_inc(x2l_ready, 1)
                        if kind == "LG":
                            dve.wait_ge(lg_mm, n + 1)
                            nc.vector.tensor_copy(logits[:, n, :], A7[:, 0:E]).then_inc(lg_ready, 1)
                if b < B:
                    ots_copy(b, 3)
            def bc(v, n):
                return v.unsqueeze(2).broadcast_to([P, v.shape[1], n])

            dve.wait_ge(lg_ready, TT)
            dve.wait_ge(rconst_ready, 5)
            prev = logits
            for c, m in ((0, r_m1), (1, r_m2)):
                step(nc.vector.tensor_reduce(m, prev, AX.X, ALU.max))
                if c == 1:
                    nc.vector.tensor_tensor(r_diff, r_m2, r_m1, ALU.subtract).then_inc(route_d, 1)
                step(nc.vector.tensor_tensor(r_eq, prev, bc(m, E), ALU.is_equal))
                step(nc.vector.tensor_tensor(r_key, r_eq, r_rank, ALU.mult))
                step(nc.vector.tensor_reduce(r_top, r_key, AX.X, ALU.max))
                step(nc.vector.tensor_tensor(r_oh[c], r_key, bc(r_top, E), ALU.is_equal))
                if c == 0:
                    step(nc.vector.scalar_tensor_tensor(out=r_two, in0=r_oh[0], scalar=-3.0e38, in1=logits, op0=ALU.mult, op1=ALU.add))
                    prev = r_two
            nc.vector.tensor_tensor(r_mask.rearrange("p e t -> p t e"), r_oh[0], r_oh[1], ALU.add).then_inc(route_m, 1)
            nc.vector.memset(r_one8, 1.0).then_inc(dve_step, 1)
            count[0] += 1
            step(nc.vector.memset(r_reset.rearrange("p e t -> p (e t)"), 1.0))
            step(nc.vector.memset(r_reset[:, :, 0:1], 0.0))
            dve.wait_ge(route_a, 1)
            step(nc.vector.tensor_scalar(r_w[:, 0:TT], r_exp, 1.0, None, ALU.add))
            step(nc.vector.reciprocal(r_w[:, 0:TT], r_w[:, 0:TT]))
            step(nc.vector.tensor_tensor(r_w[:, TT:2 * TT], r_exp, r_w[:, 0:TT], ALU.mult))
            step(nc.vector.tensor_copy(r_wh, r_w))
            step(nc.vector.tensor_tensor(r_wl, r_w, r_wh, ALU.subtract))
            dve.wait_ge(route_mm, 1)
            flat = lambda v: v.rearrange("p e t -> p (e t)")
            step(nc.vector.tensor_copy(flat(r_tot), bank[1][:, 0:P]))
            step(nc.vector.tensor_tensor_scan(flat(r_inc), flat(r_reset), flat(r_tot), 0.0, ALU.mult, ALU.add))
            step(nc.vector.tensor_tensor(flat(r_slot), flat(r_inc), flat(r_tot), ALU.subtract))
            step(nc.vector.tensor_tensor(flat(r_slot), flat(r_slot), bank[0][:, 0:P], ALU.add))
            step(nc.vector.tensor_scalar(r_cnti, r_inc[:, :, TT - 1], float(P - 1), None, ALU.add))
            step(nc.vector.tensor_single_scalar(r_cntj, r_cnti, 7, ALU.arith_shift_right))
            step(nc.vector.tensor_copy(r_nt, r_cntj))
            step(nc.vector.tensor_tensor_scan(r_end, r_one8, r_nt, 0.0, ALU.mult, ALU.add))
            step(nc.vector.tensor_tensor(r_base, r_end, r_nt, ALU.subtract))
            step(nc.vector.tensor_scalar(r_base, r_base, float(P), None, ALU.mult))
            step(nc.vector.tensor_tensor(r_slot, r_slot, bc(r_base, TT), ALU.add))
            for c in range(2):
                step(nc.vector.tensor_tensor(r_key, r_oh[c], r_slot.rearrange("p e t -> p t e"), ALU.mult))
                step(nc.vector.tensor_reduce(r_sl[:, c * TT:(c + 1) * TT], r_key, AX.X, ALU.add))
            step(nc.vector.tensor_copy(r_sli, r_sl))
            step(nc.vector.tensor_single_scalar(r_tilei, r_sli, 7, ALU.arith_shift_right))
            step(nc.vector.tensor_single_scalar(r_posi, r_sli, P - 1, ALU.bitwise_and))
            step(nc.vector.tensor_copy(r_tile, r_tilei))
            step(nc.vector.tensor_copy(r_pos, r_posi))
            J = 2 * TT
            step(nc.vector.tensor_tensor(oneh, r_iota.unsqueeze(1).broadcast_to([P, J, P]), bc(r_pos, P), ALU.is_equal))
            step(nc.vector.tensor_tensor(rtab[:, :, 0, :], r_iota[:, 0:NTP].unsqueeze(1).broadcast_to([P, J, NTP]), bc(r_tile, NTP), ALU.is_equal))
            for c in range(2):
                h = slice(c * TT, (c + 1) * TT)
                step(nc.vector.tensor_tensor(rtab[:, h, 1, :], rtab[:, h, 0, :], bc(r_tok, NTP), ALU.mult))
            step(nc.vector.tensor_tensor(rtab[:, :, 2, :], rtab[:, :, 0, :], bc(r_wh, NTP), ALU.mult))
            nc.vector.tensor_tensor(rtab[:, :, 3, :], rtab[:, :, 0, :], bc(r_wl, NTP), ALU.mult).then_inc(route_t, 1)
            cmp = rcmp.rearrange("p (i e) -> p i e", e=E)
            step(nc.vector.tensor_tensor(cmp, bc(r_iota[:, 0:NTP], E), r_end.unsqueeze(1).broadcast_to([P, NTP, E]), ALU.is_ge))
            step(nc.vector.tensor_reduce(r_exf, cmp, AX.X, ALU.add))
            step(nc.vector.tensor_scalar(tile_exp[:, :], r_exf[0:1, :], float(E - 1), None, ALU.min))
            dve.wait_ge(route_mm, 2)
            step(nc.vector.tensor_copy(r_tab.rearrange("p k n -> p (k n)"), bank[2][:, 0:4 * NTP]))
            step(nc.vector.tensor_scalar(r_free, r_tab[:, 0, :], -1.0, 1.0, ALU.mult, ALU.add))
            step(nc.vector.scalar_tensor_tensor(out=slot_tok[:, :], in0=r_free, scalar=r_pad[:, 0:1], in1=r_tab[:, 1, :], op0=ALU.mult, op1=ALU.add))
            nc.vector.tensor_tensor(slot_w[:, :], r_tab[:, 2, :], r_tab[:, 3, :], ALU.add).then_inc(idx_ready, 1)

            for n in range(EARLY * NCH, E * NCH):
                if on_dve(n):
                    _, hi, lo = piece(n)
                    dve.wait_ge(w_hi, n + 1)
                    nc.vector.tensor_tensor(lo, stage[place(n)], hi, ALU.subtract).then_inc(w_lo_dve, 1)

            def hidden(k, n):
                dve.wait_ge(sil_ready, k + 1)
                nc.vector.tensor_tensor(sil, sil, bank[2 * n + 1][:, :], ALU.mult).then_inc(h_ready, 1)
                dve.wait_ge(hi_ready, k + 1)
                nc.vector.tensor_tensor(hs[n][:, 1, :], sil, hs[n][:, 0, :], ALU.subtract).then_inc(lo_ready, 1)

            def result(i):
                dve.wait_ge(y_mm, i + 1)
                if not at_start(16 * i):
                    dve.wait_ge(y_out, 16 * i)
                nc.vector.tensor_scalar(y_sb, A7[:, 0:D], slot_w[:, bass.ds(i, 1)], None, ALU.mult).then_inc(y_ready, 1)

            def turn(i, first=False):
                hidden(2 * i, 0)
                hidden(2 * i + 1, 1)
                if not first:
                    result(i - 1)

            turn(0, first=True)
            turn(1)
            turn(2)
            with dve.Fori(1, (NT - 3) // 2) as j:
                turn(2 * j + 1)
                turn(2 * j + 2)
            turn(NT - 2)
            turn(NT - 1)
            result(NT - 1)

        @block.tensor
        def _(pe):
            taken = {6: None, 7: None}

            def bank_for(n, sem_name, value):
                if taken[n]:
                    pe.wait_ge(*taken[n])
                taken[n] = (sem_name, value)
                return bank[n]

            pe.wait_ge(kvw_in, 16 * 2 * KC)
            pe.wait_ge(ctx_in, 16 * KC)
            w = B * SK // 2
            for m in range(4):
                if m - 1 > 0:
                    pe.wait_ge(kl_ready, m - 1)
                for n in range(2):
                    for k in range(KC):
                        ins = nc.tensor.matmul(bank[2 * (m % 2) + n][:, 0:w], wk_sb[:, k, m * P:(m + 1) * P], ctx_sb[:, k, n * w:(n + 1) * w],
                                               start=(k == 0), stop=(k == KC - 1))
                ins.then_inc(kv_mm, 1)
            pe.wait_ge(const_ready, 6)
            def transposed_x(b):
                pe.wait_ge(xn_ready, TPB * (b + 1))
                A = bank_for(6, xnT_ready, b + 1)
                for k in range(KC):
                    for t in range(TPB):
                        ins = nc.tensor.transpose(A[:, k * S + t * P:k * S + (t + 1) * P], xn[:, t, k * P:(k + 1) * P], identf)
                ins.then_inc(xt_mm, 1)

            def queries(b):
                pe.wait_ge(wq_in, 16 * KC)
                pe.wait_ge(xnT_ready, b + 1)
                for a in range(2):
                    A = bank_for(6 + a, ql_ready, 2 * b + a + 1)
                    for half in range(2):
                        m = 2 * a + half
                        for k in range(KC):
                            ins = nc.tensor.matmul(A[:, half * S:(half + 1) * S], wq_sb[:, k, m * P:(m + 1) * P], xnT[:, k, :],
                                                   start=(k == 0), stop=(k == KC - 1))
                    ins.then_inc(q_mm, 1)

            def scores_for_max(b, g):
                t, heads = score_group(g)
                if g == 0:
                    pe.wait_ge(qst_in[b % 2], 32 * (b // 2 + 1))
                    pe.wait_ge(kst_in[b % 2], 32 * (b // 2 + 1))
                    pe.wait_ge(kl_ready, 4)
                if 12 * b + g - 1 > 0:
                    pe.wait_ge(mx_ready, 12 * b + g - 1)
                for n, h in enumerate(heads):
                    ins = nc.tensor.matmul(sc_bank[g % 2][:, 2 * SK * n:2 * SK * (n + 1)], qst[b % 2][:, h, t * P:(t + 1) * P], kst[b % 2][:, h, :],
                                           start=True, stop=True)
                ins.then_inc(sc_mm, 1)

            def transposed_max(b):
                pe.wait_ge(mneg_ready, TPB * (b + 1))
                A = bank_for(6, mT_ready, b + 1)
                for t in range(TPB):
                    ins = nc.tensor.transpose(A[0:64, t * 64:(t + 1) * 64].bitcast(BF16), mneg[:, t].rearrange("p a s h -> p (a s h)"), ident[:, :])
                ins.then_inc(mt_mm, 1)

            def scores(b, h):
                n = H * b + h
                if h == 0:
                    pe.wait_ge(m_in, 32 * (b + 1))
                if n - 1 > 0:
                    pe.wait_ge(p_ready, n - 1)
                for a in range(2):
                    ins = nc.tensor.matmul(st_bank[h % 2][0:SK, a * S:(a + 1) * S], kst[b % 2][:, h, a * SK:(a + 1) * SK], qst[b % 2][:, h, :],
                                           start=True, stop=True)
                ins.then_inc(st_mm, 1)

            def weighted_values(b, h):
                n, g = H * b + h, h // 4
                if n == 0:
                    pe.wait_ge(v_ready, B)
                if h % 4 == 0:
                    if 4 * b + g - 1 > 0:
                        pe.wait_ge(ots_ready, 4 * b + g - 1)
                pe.wait_ge(p_ready, n + 1)
                q = 32 * (h % 4)
                nc.tensor.matmul(ot_bank[g % 2][q:q + 32, :], vp[0:SK, b, h * VW:h * VW + 32], pr[h % 2][0:SK, :],
                                 start=True, stop=True).then_inc(pv_mm, 1)

            def heads_to_tokens(n, i):
                pe.wait_ge(ots_ready, 4 * (n // TPB) + 4)
                for a in range(2):
                    A = bank_for(6 + a, o_ready, n + 1)
                    for g in range(4):
                        c = a * S + i * P
                        ins = nc.tensor.transpose(A[:, g * P:(g + 1) * P], ots[:, g, c:c + P], identf)
                ins.then_inc(dt_mm, 1)

            def turned(src, src_sem, n, done, taken_by):
                pe.wait_ge(src_sem, n + 1)
                A = bank_for(6, taken_by, n + 1)
                for k in range(KC):
                    ins = nc.tensor.transpose(A[:, k * P:(k + 1) * P], src[:, k * P:(k + 1) * P], identf)
                ins.then_inc(done, 1)

            def product(src, src_sem, n, weights, width, done, taken_by):
                pe.wait_ge(src_sem, n + 1)
                A = bank_for(7, taken_by, n + 1)
                for k in range(KC):
                    ins = nc.tensor.matmul(A[:, 0:width], src[:, k * P:(k + 1) * P], weights[:, k, :], start=(k == 0), stop=(k == KC - 1))
                ins.then_inc(done, 1)

            transposed_x(0)
            queries(0)
            for b in range(B):
                if b - 1 > 0:
                    pe.wait_ge(v_ready, b - 1)
                for k in range(KC):
                    ins = nc.tensor.matmul(ot_bank[b % 2][0:SK, 0:D], ctx_sb[:, k, b * SK:(b + 1) * SK], wv_sb[:, k, :],
                                           start=(k == 0), stop=(k == KC - 1))
                ins.then_inc(v_mm, 1)
            transposed_x(1)
            queries(1)
            pe.wait_ge(setup_dve, 6)
            pe.wait_ge(smalls_in, 16 * 9)
            for g in range(12):
                scores_for_max(0, g)
            transposed_max(0)
            scores(0, 0)
            for b in range(B + 1):
                for h in range(H):
                    if b < B and (b, h) != (B - 1, H - 1):
                        scores(b + (h + 1) // H, (h + 1) % H)
                    for kind, i, bb in steps(b, h):
                        n = TPB * bb + i
                        if kind == "XT":
                            transposed_x(bb)
                        if kind == "Q":
                            queries(bb)
                        if kind == "SC":
                            scores_for_max(bb, i)
                        if kind == "MT":
                            transposed_max(bb)
                        if kind == "DT":
                            heads_to_tokens(n, i)
                        if kind == "OT":
                            turned(o_sb[:, i, :], o_ready, n, otr_mm, oT_ready)
                        if kind == "PJ":
                            product(oT, oT_ready, n, pj_sb, D, pj_mm, xm1_ready)
                        if kind == "X2":
                            turned(x2[:, i, :], x2_ready, n, x2t_mm, x2T_ready)
                        if kind == "LG":
                            product(x2T, x2T_ready, n, gate_sb, E, lg_mm, lg_ready)
                    if b < B:
                        weighted_values(b, h)

            pe.wait_ge(route_m, 1)
            mask = r_mask.rearrange("p e t -> p (e t)")
            nc.tensor.matmul(bank[0][:, 0:P], r_before, mask, start=True, stop=True)
            nc.tensor.matmul(bank[1][:, 0:P], r_ones, mask, start=True, stop=True).then_inc(route_mm, 1)
            pe.wait_ge(route_t, 1)
            for j in range(2 * TT):
                ins = nc.tensor.matmul(bank[2][:, 0:4 * NTP], oneh[:, j, :], rtab[:, j].rearrange("p k n -> p (k n)"),
                                       start=(j == 0), stop=(j == 2 * TT - 1))
            ins.then_inc(route_mm, 1)

            wf = WE[:, :, :].rearrange("p e n -> p (e n)")

            def turned_rows(i, p):
                pe.wait_ge(xg_in[p], 16 * ((i - p) // 2 + 1) if isinstance(i, int) else 8 * (i - p) + 16)
                if not at_start(i):
                    pe.wait_ge(xgT_ready, i)
                A = A6[:, 0:256].bitcast(BF16)
                for c in range(4):
                    ins = nc.tensor.transpose(A[:, c * P:(c + 1) * P], xg[p][:, c * P:(c + 1) * P], ident[:, :])
                ins.then_inc(xgt_mm, 1)

            def up(i, p, n, at):
                k = 2 * i + n
                if n == 0:
                    pe.wait_ge(xgT_ready, i + 1)
                if not at_start(k - 1):
                    pe.wait_ge(sil_ready, k - 1)
                if not at_start(k - 1):
                    pe.wait_ge(h_ready, k - 1)
                terms = [(part, kc, wpart) for kc in range(KC) for part, wparts in ((0, (0, 1)), (1, (0,))) for wpart in wparts]
                for z, (part, kc, wpart) in enumerate(terms):
                    for gu in range(2):
                        o = wpart * W1N + kc * 2 * FF + gu * FF + n * 512
                        ins = nc.tensor.matmul(bank[2 * n + gu][:, :], xgT[p][:, 2 * part + kc, :], wf[:, bass.ds(at + o, 512)],
                                               start=(z == 0), stop=(z == len(terms) - 1))
                ins.then_inc(g_mm, 1)

            def turned_hidden(k, n):
                pe.wait_ge(lo_ready, k + 1)
                if not at_start(k - 1):
                    pe.wait_ge(hT_ready, k - 1)
                A = bank[4 + n][:, :].bitcast(BF16)
                for c in range(8):
                    ins = nc.tensor.transpose(A[:, c * P:(c + 1) * P], hs[n][:, c // 4, (c % 4) * P:(c % 4 + 1) * P], ident[:, :])
                ins.then_inc(ht_mm, 1)

            def down(i, at):
                pe.wait_ge(hT_ready, 2 * i + 2)
                if not at_start(i):
                    pe.wait_ge(y_ready, i)
                terms = [(c, part, wpart) for c in range(FC) for part, wpart in ((0, 0), (0, 1), (1, 0))]
                for z, (c, part, wpart) in enumerate(terms):
                    o = 2 * W1N + wpart * W2N + c * D
                    ins = nc.tensor.matmul(A7[:, 0:D], hT[c // 4][:, 4 * part + c % 4, :], wf[:, bass.ds(at + o, D)],
                                           start=(z == 0), stop=(z == len(terms) - 1))
                ins.then_inc(y_mm, 1)

            def weights_at(i):
                e = pe.value_load(tile_exp[0:1, bass.ds(i, 1)], min_val=0, max_val=E - 1)
                return pe.snap(e * EW)

            def turn(i, p, first=False, last=False):
                at = weights_at(i)
                up(i, p, 0, at)
                if not first:
                    turned_hidden(2 * i - 1, 1)
                if not last:
                    turned_rows(i + 1, 1 - p)
                up(i, p, 1, at)
                if not first:
                    down(i - 1, weights_at(i - 1))
                turned_hidden(2 * i, 0)

            pe.wait_ge(idx_ready, 1)
            pe.wait_ge(w_lo_dve, lows(E * NCH - 1, True))
            pe.wait_ge(w_lo, lows(E * NCH - 1, False))
            turned_rows(0, 0)
            turn(0, 0, first=True)
            turn(1, 1)
            turn(2, 0)
            with pe.Fori(1, (NT - 3) // 2) as j:
                turn(2 * j + 1, 1)
                turn(2 * j + 2, 0)
            turn(NT - 2, 1)
            turn(NT - 1, 0, last=True)
            turned_hidden(2 * NT - 1, 1)
            down(NT - 1, weights_at(NT - 1))


_SHAPES = {"x": (T, D), "ctxT": (D, B * SK), "wqT": (D, 2 * D), "wkT": (D, 2 * D), "wvT": (D, D), "projT": (D, D),
           "proj_b": (D,), "norm_w": (D, 1), "lam1": (H,), "lam2": (H,), "gateT": (D, E), "w1": (E, P, W1N), "w2": (E, P, W2N)}


def kernel(**inputs):
    import concourse.bacc as _bacc
    from concourse.bass_utils import run_bass_kernel_spmd as _run

    a = {k: np.asarray(v) for k, v in inputs.items()}
    cont = np.ascontiguousarray
    kv1, kv2 = a["L0_xattn_kv1_w"], a["L0_xattn_kv2_w"]

    def by_half(w1, w2):
        return np.stack([w1, w2]).reshape(2, H // 2, 2, HD, D).transpose(4, 0, 2, 1, 3).reshape(D, 2 * D)

    arrays = {
        "x": a["x"].reshape(T, D),
        "ctxT": a["ctx_1024"].reshape(B * SK, D).T,
        "wqT": by_half(a["L0_xattn_q1_w"], a["L0_xattn_q2_w"]),
        "wkT": by_half(kv1[:D], kv2[:D]),
        "wvT": kv1[D:].T,
        "projT": a["L0_xattn_proj_w"].T,
        "proj_b": a["L0_xattn_proj_b"],
        "norm_w": a["L0_xattn_norm_w"].reshape(D, 1),
        "lam1": a["L0_xattn_lambda_1"].reshape(H),
        "lam2": a["L0_xattn_lambda_2"].reshape(H),
        "gateT": a["L0_ffn_gate_w"].T,
        "w1": a["L0_ffn_gate_up_proj"].transpose(0, 2, 1).reshape(E, KC, P, 2 * FF).transpose(0, 2, 1, 3).reshape(E, P, W1N),
        "w2": a["L0_ffn_down_proj"].transpose(0, 2, 1).reshape(E, FC, P, D).transpose(0, 2, 1, 3).reshape(E, P, W2N),
    }
    nc = _bacc.Bacc("TRN2", target_bir_lowering=False, num_devices=1)
    args = [nc.dram_tensor(n, shape, F32, kind="ExternalInput").ap() for n, shape in _SHAPES.items()]
    out = nc.dram_tensor("out", (T + P, D), F32, kind="ExternalOutput").ap()
    moe_attention_kernel(nc, *args, out)
    r = _run(nc, [{k: cont(v) for k, v in arrays.items()}], core_ids=[0])
    return r.results[0]["out"][:T].reshape(B, S, D)
```
